# Optimizing a Trainium2 kernel written in Bass

```python
import numpy as np
import jax
import jax.numpy as jnp

def _softmax(x, axis=-1):
    return jax.nn.softmax(x, axis=axis)

def _gelu(x):
    return jax.nn.gelu(x, approximate=True)

def _silu(x):
    return jax.nn.silu(x)

def _sigmoid(x):
    return jax.nn.sigmoid(x)

def _layernorm(x, axis=-1, eps=1e-05):
    m = jnp.mean(x, axis=axis, keepdims=True)
    v = jnp.var(x, axis=axis, keepdims=True)
    return (x - m) / jnp.sqrt(v + eps)

def _scatter_add(tgt, idx, src, axis=0):
    return tgt.at[idx].add(src)

def _segment_sum(src, seg, n):
    return jax.ops.segment_sum(src, seg, n)
kernel_name = 'mk_conv_preact_d4_conv_nhwc768_r4_5d7ad4'

def setup_inputs(seed: int=0):
    np.random.seed(seed)
    _w = jnp.asarray

    def _rec_inputs():
        import jax
        import jax.numpy as jnp
        _gk = jax.random.key(seed)
        x = -0.0001538 + 1 * jax.random.normal(jax.random.fold_in(_gk, 1), (8, 32, 32, 192), jnp.float32)
        return x
    x = _rec_inputs()

    def _L0_conv_setup():
        import jax, jax.numpy as jnp
        import numpy as np
        NUM_HEADS = 12

        def _rel_lookup(rel_pos, size):
            idx = jnp.arange(size)[:, None] - jnp.arange(size)[None, :] + (size - 1)
            return rel_pos[idx]
        key = jax.random.key(seed)
        ks = jax.random.split(key, 7)
        B, H, W, C = (8, 32, 32, 192)
        return {'x': jax.random.normal(ks[0], (B, H, W, C), dtype=jnp.float32), 'w_qkv': jax.random.normal(ks[1], (C, 3 * C), dtype=jnp.float32) * 0.02, 'b_qkv': jax.random.normal(ks[2], (3 * C,), dtype=jnp.float32) * 0.02, 'w_proj': jax.random.normal(ks[3], (C, C), dtype=jnp.float32) * 0.02, 'b_proj': jax.random.normal(ks[4], (C,), dtype=jnp.float32) * 0.02, 'rel_pos_h': jax.random.normal(ks[5], (2 * H - 1, C // NUM_HEADS), dtype=jnp.float32) * 0.02, 'rel_pos_w': jax.random.normal(ks[6], (2 * W - 1, C // NUM_HEADS), dtype=jnp.float32) * 0.02}
    _L0_conv_all = _L0_conv_setup()
    _L0_conv_in = {k: v for k, v in _L0_conv_all.items() if k in ('w_qkv', 'b_qkv', 'w_proj', 'b_proj', 'rel_pos_h', 'rel_pos_w')}
    del _L0_conv_all

    def _L1_conv_setup():
        import jax, jax.numpy as jnp
        import numpy as np
        D_MODEL = 192
        D_HEAD = 16
        N_HEADS = D_MODEL // D_HEAD
        KERNEL = 7
        NEG_INF = -1e+30

        def make_neighbourhood_mask(kernel_h, kernel_w, canvas_h, canvas_w):
            h_ramp = jnp.arange(canvas_h)
            w_ramp = jnp.arange(canvas_w)
            h_pos, w_pos = jnp.meshgrid(h_ramp, w_ramp, indexing='ij')
            start_h = jnp.clip(h_pos - kernel_h // 2, 0, canvas_h - kernel_h)[..., None, None]
            end_h = start_h + kernel_h
            start_w = jnp.clip(w_pos - kernel_w // 2, 0, canvas_w - kernel_w)[..., None, None]
            end_w = start_w + kernel_w
            h_range = h_ramp.reshape(1, 1, canvas_h, 1)
            w_range = w_ramp.reshape(1, 1, 1, canvas_w)
            mask = (h_range >= start_h) & (h_range < end_h) & (w_range >= start_w) & (w_range < end_w)
            return mask.reshape(canvas_h * canvas_w, canvas_h * canvas_w)
        key = jax.random.key(seed)
        k1, k2, k3, k4, k5, k6 = jax.random.split(key, 6)
        x = jax.random.normal(k1, (2, 48, 48, D_MODEL), dtype=jnp.float32)
        registers = jax.random.normal(k2, (16, D_MODEL), dtype=jnp.float32)
        scale = 1.0 / np.sqrt(D_MODEL)
        qkv_w = jax.random.normal(k3, (3 * D_MODEL, D_MODEL), dtype=jnp.float32) * scale
        qkv_b = jax.random.normal(k4, (3 * D_MODEL,), dtype=jnp.float32) * 0.01
        out_w = jax.random.normal(k5, (D_MODEL, D_MODEL), dtype=jnp.float32) * scale
        out_b = jax.random.normal(k6, (D_MODEL,), dtype=jnp.float32) * 0.01
        return {'x': x, 'registers': registers, 'qkv_w': qkv_w, 'qkv_b': qkv_b, 'out_w': out_w, 'out_b': out_b}
    _L1_conv_all = _L1_conv_setup()
    _L1_conv_in = {k: v for k, v in _L1_conv_all.items() if k in ('registers', 'qkv_w', 'qkv_b', 'out_w', 'out_b')}
    del _L1_conv_all

    def _L2_conv_setup():
        import jax, jax.numpy as jnp
        import numpy as np
        B, H, W, DIM, NH = (8, 32, 32, 192, 12)
        HD = DIM // NH

        def _get_rel(rel_pos, size):
            idx = jnp.arange(size)[:, None] - jnp.arange(size)[None, :] + (size - 1)
            return rel_pos[idx]
        key = jax.random.key(seed)
        ks = jax.random.split(key, 7)
        x = jax.random.normal(ks[0], (B, H, W, DIM), dtype=jnp.float32)
        qkv_w = jax.random.normal(ks[1], (3 * DIM, DIM), dtype=jnp.float32) * 0.02
        qkv_b = jax.random.normal(ks[2], (3 * DIM,), dtype=jnp.float32) * 0.02
        proj_w = jax.random.normal(ks[3], (DIM, DIM), dtype=jnp.float32) * 0.02
        proj_b = jax.random.normal(ks[4], (DIM,), dtype=jnp.float32) * 0.02
        rel_pos_h = jax.random.normal(ks[5], (2 * H - 1, HD), dtype=jnp.float32) * 0.02
        rel_pos_w = jax.random.normal(ks[6], (2 * W - 1, HD), dtype=jnp.float32) * 0.02
        return {'x': x, 'qkv_w': qkv_w, 'qkv_b': qkv_b, 'proj_w': proj_w, 'proj_b': proj_b, 'rel_pos_h': rel_pos_h, 'rel_pos_w': rel_pos_w}
    _L2_conv_all = _L2_conv_setup()
    _L2_conv_in = {k: v for k, v in _L2_conv_all.items() if k in ('qkv_w', 'qkv_b', 'proj_w', 'proj_b', 'rel_pos_h', 'rel_pos_w')}
    del _L2_conv_all

    def _L3_conv_setup():
        import jax, jax.numpy as jnp
        import numpy as np

        def rotate_every_two(x):
            x1 = x[..., ::2]
            x2 = x[..., 1::2]
            return jnp.stack([-x2, x1], axis=-1).reshape(x.shape)

        def theta_shift(x, sin, cos):
            return x * cos + rotate_every_two(x) * sin
        key = jax.random.key(seed)
        ks = jax.random.split(key, 16)
        B, H, W, C, NH = (8, 32, 32, 192, 12)
        HD = C // NH
        gain = 2 ** (-2.5)
        xavier = lambda k, shp, g: jax.random.normal(k, shp, jnp.float32) * (g * (2.0 / (shp[0] + shp[1])) ** 0.5)
        return {'x': jax.random.normal(ks[0], (B, H, W, C), jnp.float32), 'sin': jax.random.normal(ks[1], (H, W, HD), jnp.float32), 'cos': jax.random.normal(ks[2], (H, W, HD), jnp.float32), 'mask': jax.random.normal(ks[3], (NH, H * W, H * W), jnp.float32), 'wq': xavier(ks[4], (C, C), gain), 'bq': jnp.zeros((C,), jnp.float32), 'wk': xavier(ks[5], (C, C), gain), 'bk': jnp.zeros((C,), jnp.float32), 'wv': xavier(ks[6], (C, C), gain), 'bv': jnp.zeros((C,), jnp.float32), 'lepe_w': jax.random.normal(ks[7], (5, 5, 1, C), jnp.float32) * 0.05, 'lepe_b': jnp.zeros((C,), jnp.float32), 'wo': xavier(ks[8], (C, C), 1.0), 'bo': jnp.zeros((C,), jnp.float32)}
    _L3_conv_all = _L3_conv_setup()
    _L3_conv_in = {k: v for k, v in _L3_conv_all.items() if k in ('sin', 'cos', 'mask', 'wq', 'bq', 'wk', 'bk', 'wv', 'bv', 'lepe_w', 'lepe_b', 'wo', 'bo')}
    del _L3_conv_all
    return {'x': x, 'L0_conv_w_qkv': _L0_conv_in['w_qkv'], 'L0_conv_b_qkv': _L0_conv_in['b_qkv'], 'L0_conv_w_proj': _L0_conv_in['w_proj'], 'L0_conv_b_proj': _L0_conv_in['b_proj'], 'L0_conv_rel_pos_h': _L0_conv_in['rel_pos_h'], 'L0_conv_rel_pos_w': _L0_conv_in['rel_pos_w'], 'L1_conv_registers': _L1_conv_in['registers'], 'L1_conv_qkv_w': _L1_conv_in['qkv_w'], 'L1_conv_qkv_b': _L1_conv_in['qkv_b'], 'L1_conv_out_w': _L1_conv_in['out_w'], 'L1_conv_out_b': _L1_conv_in['out_b'], 'L2_conv_qkv_w': _L2_conv_in['qkv_w'], 'L2_conv_qkv_b': _L2_conv_in['qkv_b'], 'L2_conv_proj_w': _L2_conv_in['proj_w'], 'L2_conv_proj_b': _L2_conv_in['proj_b'], 'L2_conv_rel_pos_h': _L2_conv_in['rel_pos_h'], 'L2_conv_rel_pos_w': _L2_conv_in['rel_pos_w'], 'L3_conv_sin': _L3_conv_in['sin'], 'L3_conv_cos': _L3_conv_in['cos'], 'L3_conv_mask': _L3_conv_in['mask'], 'L3_conv_wq': _L3_conv_in['wq'], 'L3_conv_bq': _L3_conv_in['bq'], 'L3_conv_wk': _L3_conv_in['wk'], 'L3_conv_bk': _L3_conv_in['bk'], 'L3_conv_wv': _L3_conv_in['wv'], 'L3_conv_bv': _L3_conv_in['bv'], 'L3_conv_lepe_w': _L3_conv_in['lepe_w'], 'L3_conv_lepe_b': _L3_conv_in['lepe_b'], 'L3_conv_wo': _L3_conv_in['wo'], 'L3_conv_bo': _L3_conv_in['bo']}

def reference(x, L0_conv_w_qkv, L0_conv_b_qkv, L0_conv_w_proj, L0_conv_b_proj, L0_conv_rel_pos_h, L0_conv_rel_pos_w, L1_conv_registers, L1_conv_qkv_w, L1_conv_qkv_b, L1_conv_out_w, L1_conv_out_b, L2_conv_qkv_w, L2_conv_qkv_b, L2_conv_proj_w, L2_conv_proj_b, L2_conv_rel_pos_h, L2_conv_rel_pos_w, L3_conv_sin, L3_conv_cos, L3_conv_mask, L3_conv_wq, L3_conv_bq, L3_conv_wk, L3_conv_bk, L3_conv_wv, L3_conv_bv, L3_conv_lepe_w, L3_conv_lepe_b, L3_conv_wo, L3_conv_bo):
    import jax
    import jax.numpy as jnp

    def _L0_conv_ref(x, w_qkv, b_qkv, w_proj, b_proj, rel_pos_h, rel_pos_w):
        import jax, jax.numpy as jnp
        import numpy as np
        NUM_HEADS = 12

        def _rel_lookup(rel_pos, size):
            idx = jnp.arange(size)[:, None] - jnp.arange(size)[None, :] + (size - 1)
            return rel_pos[idx]
        B, H, W, C = x.shape
        nh = NUM_HEADS
        hd = C // nh
        scale = hd ** (-0.5)
        qkv = x @ w_qkv + b_qkv
        qkv = qkv.reshape(B, H * W, 3, nh, hd).transpose(2, 0, 3, 1, 4)
        qkv = qkv.reshape(3, B * nh, H * W, hd)
        q, k, v = (qkv[0], qkv[1], qkv[2])
        attn = jnp.einsum('bqd,bkd->bqk', q * scale, k)
        Rh = _rel_lookup(rel_pos_h, H)
        Rw = _rel_lookup(rel_pos_w, W)
        r_q = q.reshape(B * nh, H, W, hd)
        rel_h = jnp.einsum('bhwc,hkc->bhwk', r_q, Rh)
        rel_w = jnp.einsum('bhwc,wkc->bhwk', r_q, Rw)
        attn = (attn.reshape(B * nh, H, W, H, W) + rel_h[:, :, :, :, None] + rel_w[:, :, :, None, :]).reshape(B * nh, H * W, H * W)
        attn = jax.nn.softmax(attn, axis=-1)
        out = jnp.einsum('bqk,bkd->bqd', attn, v)
        out = out.reshape(B, nh, H, W, hd).transpose(0, 2, 3, 1, 4).reshape(B, H, W, C)
        return out @ w_proj + b_proj

    def _L1_conv_ref(x, registers, qkv_w, qkv_b, out_w, out_b):
        import jax, jax.numpy as jnp
        import numpy as np
        D_MODEL = 192
        D_HEAD = 16
        N_HEADS = D_MODEL // D_HEAD
        KERNEL = 7
        NEG_INF = -1e+30

        def make_neighbourhood_mask(kernel_h, kernel_w, canvas_h, canvas_w):
            h_ramp = jnp.arange(canvas_h)
            w_ramp = jnp.arange(canvas_w)
            h_pos, w_pos = jnp.meshgrid(h_ramp, w_ramp, indexing='ij')
            start_h = jnp.clip(h_pos - kernel_h // 2, 0, canvas_h - kernel_h)[..., None, None]
            end_h = start_h + kernel_h
            start_w = jnp.clip(w_pos - kernel_w // 2, 0, canvas_w - kernel_w)[..., None, None]
            end_w = start_w + kernel_w
            h_range = h_ramp.reshape(1, 1, canvas_h, 1)
            w_range = w_ramp.reshape(1, 1, 1, canvas_w)
            mask = (h_range >= start_h) & (h_range < end_h) & (w_range >= start_w) & (w_range < end_w)
            return mask.reshape(canvas_h * canvas_w, canvas_h * canvas_w)
        n, h, w, _ = x.shape
        nh, e = (N_HEADS, D_HEAD)
        s = h * w
        r = registers.shape[0]
        qkv = x @ qkv_w.T + qkv_b
        qkv = qkv.reshape(n, h, w, 3, nh, e)
        qkv = qkv.transpose(3, 0, 4, 1, 2, 5).reshape(3, n, nh, s, e)
        q, k, v = (qkv[0], qkv[1], qkv[2])
        reg_kv = registers @ qkv_w[D_MODEL:].T + qkv_b[D_MODEL:]
        reg_kv = reg_kv.reshape(r, 2, nh, e).transpose(1, 2, 0, 3)
        reg_k = jnp.broadcast_to(reg_kv[0][None], (n, nh, r, e))
        reg_v = jnp.broadcast_to(reg_kv[1][None], (n, nh, r, e))
        k_cat = jnp.concatenate([k, reg_k], axis=-2)
        v_cat = jnp.concatenate([v, reg_v], axis=-2)
        mask = make_neighbourhood_mask(KERNEL, KERNEL, h, w)
        mask_cat = jnp.concatenate([mask, jnp.ones((s, r), dtype=bool)], axis=-1)
        scale = 1.0 / jnp.sqrt(jnp.asarray(e, dtype=x.dtype))
        scores = jnp.einsum('bnqe,bnke->bnqk', q, k_cat) * scale
        scores = jnp.where(mask_cat[None, None], scores, NEG_INF)
        attn = jax.nn.softmax(scores, axis=-1)
        o = jnp.einsum('bnqk,bnke->bnqe', attn, v_cat)
        o = o.transpose(0, 2, 1, 3).reshape(n, h, w, nh * e)
        return o @ out_w.T + out_b

    def _L2_conv_ref(x, qkv_w, qkv_b, proj_w, proj_b, rel_pos_h, rel_pos_w):
        import jax, jax.numpy as jnp
        import numpy as np
        B, H, W, DIM, NH = (8, 32, 32, 192, 12)
        HD = DIM // NH

        def _get_rel(rel_pos, size):
            idx = jnp.arange(size)[:, None] - jnp.arange(size)[None, :] + (size - 1)
            return rel_pos[idx]
        b, h, w, c = x.shape
        scale = HD ** (-0.5)
        qkv = x @ qkv_w.T + qkv_b
        qkv = qkv.reshape(b, h * w, 3, NH, HD).transpose(2, 0, 3, 1, 4)
        qkv = qkv.reshape(3, b * NH, h * w, HD)
        q, k, v = (qkv[0], qkv[1], qkv[2])
        attn = jnp.einsum('bqc,bkc->bqk', q * scale, k)
        Rh = _get_rel(rel_pos_h, h)
        Rw = _get_rel(rel_pos_w, w)
        r_q = q.reshape(b * NH, h, w, HD)
        rel_h = jnp.einsum('bhwc,hkc->bhwk', r_q, Rh)
        rel_w = jnp.einsum('bhwc,wkc->bhwk', r_q, Rw)
        attn = (attn.reshape(b * NH, h, w, h, w) + rel_h[:, :, :, :, None] + rel_w[:, :, :, None, :]).reshape(b * NH, h * w, h * w)
        attn = jax.nn.softmax(attn, axis=-1)
        out = attn @ v
        out = out.reshape(b, NH, h, w, HD).transpose(0, 2, 3, 1, 4).reshape(b, h, w, c)
        return out @ proj_w.T + proj_b

    def _L3_conv_ref(x, sin, cos, mask, wq, bq, wk, bk, wv, bv, lepe_w, lepe_b, wo, bo):
        import jax, jax.numpy as jnp
        import numpy as np

        def rotate_every_two(x):
            x1 = x[..., ::2]
            x2 = x[..., 1::2]
            return jnp.stack([-x2, x1], axis=-1).reshape(x.shape)

        def theta_shift(x, sin, cos):
            return x * cos + rotate_every_two(x) * sin
        B, H, W, C = x.shape
        NH = mask.shape[0]
        scaling = (C // NH) ** (-0.5)
        q = x @ wq.T + bq
        k = (x @ wk.T + bk) * scaling
        v = x @ wv.T + bv
        lepe = jax.lax.conv_general_dilated(v, lepe_w, window_strides=(1, 1), padding=[(2, 2), (2, 2)], dimension_numbers=('NHWC', 'HWIO', 'NHWC'), feature_group_count=C) + lepe_b
        qh = q.reshape(B, H, W, NH, -1).transpose(0, 3, 1, 2, 4)
        kh = k.reshape(B, H, W, NH, -1).transpose(0, 3, 1, 2, 4)
        qr = theta_shift(qh, sin, cos).reshape(B, NH, H * W, -1)
        kr = theta_shift(kh, sin, cos).reshape(B, NH, H * W, -1)
        vr = v.reshape(B, H, W, NH, -1).transpose(0, 3, 1, 2, 4).reshape(B, NH, H * W, -1)
        qk = jnp.einsum('bnld,bnmd->bnlm', qr, kr) + mask
        attn = jax.nn.softmax(qk, axis=-1)
        out = jnp.einsum('bnlm,bnmd->bnld', attn, vr)
        out = jnp.swapaxes(out, 1, 2).reshape(B, H, W, -1) + lepe
        return out @ wo.T + bo

    def _gn(v, G=32, eps=1e-05):
        B_, H_, W_, C_ = v.shape
        g = v.reshape(B_, H_, W_, G, C_ // G)
        m = jnp.mean(g, axis=(1, 2, 4), keepdims=True)
        s = jnp.var(g, axis=(1, 2, 4), keepdims=True)
        return ((g - m) / jnp.sqrt(s + eps)).reshape(v.shape)

    def _ln_c(v, eps=1e-06):
        m = jnp.mean(v, axis=-1, keepdims=True)
        s = jnp.var(v, axis=-1, keepdims=True)
        return (v - m) / jnp.sqrt(s + eps)

    def _ln_t(v, eps=1e-05):
        m = jnp.mean(v, axis=-1, keepdims=True)
        s = jnp.var(v, axis=-1, keepdims=True)
        return (v - m) / jnp.sqrt(s + eps)

    def _to_tokens(v):
        B_, H_, W_, C_ = v.shape
        return v.reshape(B_, H_ * W_, C_)

    def _from_tokens(t, like):
        return t.reshape(like.shape)
    x = x + _L0_conv_ref(_gn(x), L0_conv_w_qkv, L0_conv_b_qkv, L0_conv_w_proj, L0_conv_b_proj, L0_conv_rel_pos_h, L0_conv_rel_pos_w)
    x = x + _L1_conv_ref(_gn(x), L1_conv_registers, L1_conv_qkv_w, L1_conv_qkv_b, L1_conv_out_w, L1_conv_out_b)
    x = x + _L2_conv_ref(_gn(x), L2_conv_qkv_w, L2_conv_qkv_b, L2_conv_proj_w, L2_conv_proj_b, L2_conv_rel_pos_h, L2_conv_rel_pos_w)
    x = x + _L3_conv_ref(_gn(x), L3_conv_sin, L3_conv_cos, L3_conv_mask, L3_conv_wq, L3_conv_bq, L3_conv_wk, L3_conv_bk, L3_conv_wv, L3_conv_bv, L3_conv_lepe_w, L3_conv_lepe_b, L3_conv_wo, L3_conv_bo)
    return x

_drawn_inputs = setup_inputs


def setup_inputs(seed=0):
    import zlib

    import numpy as np

    out = dict(_drawn_inputs(seed))
    spreads = {'L3_conv_bq': (0.0, 0.8),
     'L3_conv_bk': (0.0, 0.8),
     'L3_conv_bv': (0.0, 0.347),
     'L3_conv_lepe_b': (0.0, 0.398),
     'L3_conv_bo': (0.0, 0.333)}
    factors = {'L0_conv_w_qkv': 8.0,
     'L0_conv_b_qkv': 8.0,
     'L0_conv_w_proj': 7.594,
     'L0_conv_rel_pos_h': 8.0,
     'L0_conv_rel_pos_w': 8.0,
     'L1_conv_qkv_b': 5.738,
     'L1_conv_out_b': 5.415,
     'L2_conv_qkv_w': 8.0,
     'L2_conv_qkv_b': 8.0,
     'L2_conv_proj_w': 7.16,
     'L2_conv_proj_b': 12.379,
     'L2_conv_rel_pos_h': 8.0,
     'L2_conv_rel_pos_w': 8.0,
     'L3_conv_sin': 8.0,
     'L3_conv_cos': 8.0,
     'L3_conv_wq': 8.0,
     'L3_conv_wk': 8.0,
     'L0_conv_b_proj': 4.752,
     'L3_conv_lepe_w': 5.713}
    for name, (base, spread) in spreads.items():
        noise = np.random.default_rng([zlib.crc32(name.encode()), seed]).standard_normal(out[name].shape)
        drawn = base * np.exp(spread * noise) if base else spread * noise
        out[name] = jnp.asarray(drawn.astype(out[name].dtype))
    for name, factor in factors.items():
        out[name] = (out[name] * factor).astype(out[name].dtype)
    return out
```

```python
from contextlib import ExitStack

import numpy as np

import concourse.bass as bass
from concourse import mybir

ALU = mybir.AluOpType
ACT = mybir.ActivationFunctionType
AX = mybir.AxisListType
F32 = mybir.dt.float32

P = 128
IMAGES, SIDE, CHANNELS, HEADS = 8, 32, 192, 12
TOKENS = SIDE * SIDE
DIM = CHANNELS // HEADS
GROUPS = 3
G = HEADS // GROUPS
HALF = CHANNELS // 2
CHUNKS = TOKENS // P
TILES = CHUNKS * G
Q = 32
BANK = 512
SCALE = float(DIM) ** -0.5
VW = DIM + 1
WINDOW, REGS = 7, 16
KEYS_W = 4 * P
BIG = 3.0e38
TAPS = 5
PAD = SIDE + TAPS - 1
GN_EPS = 1e-5


def alone(eng):
    eng.nop(nofuse=True)


def normalise_block(nc, sems, name, x_in, xn_out, stream_out, bias, gavg, lepe=None):
    with ExitStack() as ctx:
        def sb(n, shape):
            return ctx.enter_context(nc.sbuf_tensor(f"{name}_{n}", shape, F32))

        def sem(n):
            return sems.enter_context(nc.semaphore(f"{name}_{n}"))

        X = sb("x", [HALF, 2, TOKENS])
        XN = sb("xn", [HALF, 2, TOKENS])
        ST = sb("stream", [HALF, 2, TOKENS])
        bias_sb = sb("bias", [HALF, 2])
        gavg_sb = sb("gavg", [HALF, HALF])
        stats = sb("stats", [HALF, 2, 2, 6])
        mv = sb("mv", [HALF, 2, 2])
        sq = sb("sq", [HALF, 2])
        me = sb("me", [HALF, 2, 2])
        gm = sb("gm", [HALF, 2, 2])
        gsq = sb("gsq", [HALF, 2])
        var = sb("var", [HALF, 2])
        power = sb("power", [HALF, 2])
        rstd = sb("rstd", [HALF, 2])
        ps_g = ctx.enter_context(nc.psum_tensor(f"{name}_psg", [P, BANK], F32))
        loaded_c = sem("loaded_c")
        loaded_x = sem("loaded_x")
        stored_xn = sem("stored_xn")
        stored_st = sem("stored_st")
        power_set = sem("power_set")
        dve = sem("dve")
        averaged = sem("averaged")
        exponent_set = sem("exponent_set")
        powered = sem("powered")
        xn_ready = sem("xn_ready")
        st_ready = sem("st_ready")
        if lepe:
            VP = sb("vpad", [HALF, 2, PAD, PAD])
            CV = sb("conv", [HALF, 2, TOKENS])
            wv_sb = sb("wv", [HALF, 2, CHANNELS])
            bv_sb = sb("bv", [HALF, 2])
            lw_sb = sb("lw", [HALF, 2, TAPS * TAPS])
            lb_sb = sb("lb", [HALF, 2])
            wo_sb = sb("wo", [HALF, 2, CHANNELS])
            ps_v = ctx.enter_context(nc.psum_tensor(f"{name}_psv", [P, 4, BANK], F32))
            v_ready = sem("v_ready")
            v_padded = sem("v_padded")
            pad_set = sem("pad_set")
            taps = sem("taps")
            o_ready = sem("o_ready")
            st_added = sem("st_added")
        consts = 2 + (5 if lepe else 0)
        DVE_STEPS = 11
        NT = 2 * TAPS * TAPS
        block = ctx.enter_context(nc.Block())

        @block.sync
        def _(sp):
            sp.dma_start(bias_sb[:], bias).then_inc(loaded_c, 16)
            sp.dma_start(gavg_sb[:], gavg).then_inc(loaded_c, 16)
            if lepe:
                for dst, src in ((wv_sb, "wv"), (bv_sb, "bv"), (lw_sb, "lw"), (lb_sb, "lb"), (wo_sb, "wo")):
                    sp.dma_start(dst[:], lepe[src]).then_inc(loaded_c, 16)
            with sp.Fori(0, IMAGES) as b:
                sp.dma_start(X[:], x_in[b]).then_inc(loaded_x, 16)
                sp.wait_ge(xn_ready, 2 * b + 2)
                sp.dma_start(xn_out[b], XN[:]).then_inc(stored_xn, 16)
                sp.wait_ge(st_ready, b + 1)
                if lepe:
                    sp.wait_ge(st_added, 2 * b + 2)
                sp.dma_start(stream_out[b], ST[:]).then_inc(stored_st, 16)
            sp.wait_ge(stored_xn, 16 * IMAGES)
            sp.wait_ge(stored_st, 16 * IMAGES)

        @block.vector
        def _(eng):
            if lepe:
                nc.vector.memset(VP[:], 0.0).then_inc(pad_set, 1)
            with eng.Fori(0, IMAGES) as b:
                base = b * DVE_STEPS
                eng.wait_ge(loaded_x, 16 * b + 16)
                for m in range(2):
                    for h in range(2):
                        nc.vector.bn_stats(stats[:, m, h, :], X[:, m, h * BANK:(h + 1) * BANK]).then_inc(dve, 1)
                eng.wait_ge(dve, base + 4)
                alone(eng)
                for m in range(2):
                    nc.vector.bn_aggr(mv[:, m, :], stats[:, m, :, :].rearrange("p a b -> p (a b)")).then_inc(dve, 1)
                eng.wait_ge(dve, base + 6)
                nc.vector.tensor_tensor(sq[:], mv[:, :, 0], mv[:, :, 0], ALU.mult).then_inc(dve, 1)
                nc.vector.tensor_copy(me[:, :, 0], mv[:, :, 0]).then_inc(dve, 1)
                eng.wait_ge(dve, base + 8)
                nc.vector.tensor_tensor(me[:, :, 1], sq[:], mv[:, :, 1], ALU.add).then_inc(dve, 1)
                eng.wait_ge(averaged, b + 1)
                nc.vector.tensor_copy(gm[:], ps_g[0:HALF, 0:4].rearrange("p (a b) -> p a b", a=2)).then_inc(dve, 1)
                eng.wait_ge(dve, base + 10)
                nc.vector.tensor_tensor(gsq[:], gm[:, :, 0], gm[:, :, 0], ALU.mult).then_inc(dve, 1)
                eng.wait_ge(dve, base + 11)
                nc.vector.scalar_tensor_tensor(out=var[:], in0=gm[:, :, 1], scalar=GN_EPS, in1=gsq[:],
                                               op0=ALU.add, op1=ALU.subtract).then_inc(power_set, 1)
                eng.wait_ge(powered, b + 1)
                for m in range(2):
                    nc.vector.tensor_scalar(XN[:, m, :], X[:, m, :], gm[:, m, 0:1], rstd[:, m:m + 1],
                                            ALU.subtract, ALU.mult).then_inc(xn_ready, 1)
                if lepe:
                    eng.wait_ge(v_padded, 2 * b + 2)
                    for k in range(TAPS * TAPS):
                        dy, dx = divmod(k, TAPS)
                        for m in range(2):
                            n = NT * b + 2 * k + m
                            src = VP[:, m, dy:dy + SIDE, dx:dx + SIDE]
                            dst = CV[:, m, :].rearrange("p (a b) -> p a b", a=SIDE)
                            if k == 0:
                                ins = nc.vector.tensor_scalar(dst, src, lw_sb[:, m, 0:1], lb_sb[:, m:m + 1],
                                                              ALU.mult, ALU.add)
                            else:
                                eng.wait_ge(taps, n - 1)
                                ins = nc.vector.scalar_tensor_tensor(out=dst, in0=src, scalar=lw_sb[:, m, k:k + 1],
                                                                     in1=dst, op0=ALU.mult, op1=ALU.add)
                            ins.then_inc(taps, 1)
                    eng.wait_ge(o_ready, b + 1)
                    eng.wait_ge(st_ready, b + 1)
                    for m in range(2):
                        nc.vector.tensor_tensor(ST[:, m, :], ps_v[0:HALF, 2 * m:2 * m + 2, :].rearrange("p a b -> p (a b)"),
                                                ST[:, m, :], ALU.add).then_inc(st_added, 1)
                eng.wait_ge(stored_xn, 16 * b + 16)
                alone(eng)

        @block.tensor
        def _(pe):
            pe.wait_ge(loaded_c, 16 * consts)
            with pe.Fori(0, IMAGES) as b:
                pe.wait_ge(dve, b * DVE_STEPS + 9)
                nc.tensor.matmul(ps_g[0:HALF, 0:4], gavg_sb[:], me[:].rearrange("p a b -> p (a b)"),
                                 start=True, stop=True).then_inc(averaged, 1)
                if lepe:
                    pe.wait_ge(xn_ready, 2 * b + 2)
                    for m in range(2):
                        for t in range(2):
                            for k in range(2):
                                last = nc.tensor.matmul(ps_v[0:HALF, 2 * m + t, :], wv_sb[:, k, m * HALF:(m + 1) * HALF],
                                                        XN[:, k, t * BANK:(t + 1) * BANK], start=k == 0, stop=k == 1)
                    last.then_inc(v_ready, 1)
                    pe.wait_ge(taps, NT * b + NT)
                    pe.wait_ge(v_padded, 2 * b + 2)
                    for m in range(2):
                        for t in range(2):
                            for k in range(2):
                                last = nc.tensor.matmul(ps_v[0:HALF, 2 * m + t, :], wo_sb[:, k, m * HALF:(m + 1) * HALF],
                                                        CV[:, k, t * BANK:(t + 1) * BANK], start=k == 0, stop=k == 1)
                    last.then_inc(o_ready, 1)
                    pe.wait_ge(st_added, 2 * b + 2)
                    alone(pe)

        @block.scalar
        def _(act):
            act.wait_ge(loaded_c, 16 * consts)
            if lepe:
                act.wait_ge(pad_set, 1)
            with act.Fori(0, IMAGES) as b:
                act.wait_ge(loaded_x, 16 * b + 16)
                nc.scalar.activation(ST[:, 0, :], X[:, 0, :], ACT.Identity, bias=bias_sb[:, 0:1])
                nc.scalar.activation(ST[:, 1, :], X[:, 1, :], ACT.Identity, bias=bias_sb[:, 1:2]).then_inc(st_ready, 1)
                if lepe:
                    act.wait_ge(v_ready, b + 1)
                    for m in range(2):
                        nc.scalar.activation(VP[:, m, 2:2 + SIDE, 2:2 + SIDE],
                                             ps_v[0:HALF, 2 * m:2 * m + 2, :].rearrange("p a (y x) -> p (a y) x", x=SIDE),
                                             ACT.Identity, bias=bv_sb[:, m:m + 1]).then_inc(v_padded, 1)
                act.wait_ge(stored_st, 16 * b + 16)
                alone(act)

        @block.gpsimd
        def _(pool):
            nc.gpsimd.memset(power[:], -0.5).then_inc(exponent_set, 1)
            pool.wait_ge(exponent_set, 1)
            with pool.Fori(0, IMAGES) as b:
                pool.wait_ge(power_set, b + 1)
                nc.gpsimd.tensor_tensor(rstd[:], var[:], power[:], ALU.pow).then_inc(powered, 1)


def attend_block(nc, sems, name, kind, xn, stream_in, stream_out, w, ident, spread):
    rel, window, rotary = kind == "rel", kind == "window", kind == "rotary"
    KTOK = TOKENS + (P if window else 0)
    VC = KTOK // P
    with ExitStack() as ctx:
        def sb(n, shape):
            return ctx.enter_context(nc.sbuf_tensor(f"{name}_{n}", shape, F32))

        def sem(n):
            return sems.enter_context(nc.semaphore(f"{name}_{n}"))

        S = ctx.enter_context(nc.psum_tensor(f"{name}_S", [P, 2, 2, BANK], F32))
        PT = ctx.enter_context(nc.psum_tensor(f"{name}_PT", [P, 2, BANK], F32))
        O = ctx.enter_context(nc.psum_tensor(f"{name}_O", [P, BANK], F32))
        M = ctx.enter_context(nc.psum_tensor(f"{name}_M", [P, BANK], F32))

        def slot(s, rows=P):
            return S[0:rows, s, :, :].rearrange("p a b -> p (a b)")

        ident_sb = sb("ident", [P, P])
        spread_sb = sb("spread", [P, P])
        wo_sb = sb("wo", [P, CHANNELS])
        wv_sb = sb("wv", [HALF, 2, G * DIM])
        bv_sb = sb("bv", [G * DIM, 1])
        X = sb("X", [HALF, 2, KTOK])
        ACC = X if rotary else sb("ACC", [HALF, 2, TOKENS])
        PTS = sb("PTS", [P, 2, G, KEYS_W if window else TOKENS])
        OSB = sb("OSB", [P, TOKENS])
        VT = OSB if rotary or rel else sb("VT", [G * DIM, KTOK])
        V = sb("V", [P, VC, G, VW])
        PROB = sb("PROB", [P, 2, KEYS_W if window else TOKENS])
        nmax = sb("nmax", [P, 4])
        if rel:
            QQ = sb("QQ", [P, G, TOKENS])
            KK = sb("KK", [P, G, BANK])
            QK = sb("QK", [P, TOKENS])
            QC = sb("QC", [DIM, G, TOKENS])
            tab_h = sb("tab_h", [DIM, 2, SIDE, Q])
            tab_w = sb("tab_w", [DIM, 2 * SIDE - 1])
            weights = {"wqk": sb("wqk", [HALF, 2, P]), "bqk": sb("bqk", [P, 1])}
        else:
            QQ = sb("QQ", [P, TOKENS])
            KK = sb("KK", [P, KTOK])
            names = ["q", "k"] + (["qr", "kr"] if rotary else [])
            weights = {}
            for n in names:
                weights["w" + n] = sb("w" + n, [HALF, 2, P])
                weights["b" + n] = sb("b" + n, [P, 1])
        if window:
            mask_sb = sb("mask", [P, 3, KEYS_W])
        if rotary:
            mask_sb = sb("mask", [P, G, CHUNKS, TOKENS])
            cos_sb = sb("cos", [P, TOKENS])
            sin_sb = sb("sin", [P, TOKENS])
            sign_sb = sb("sign", [P, 1])
        weights |= {"wv": wv_sb, "bv": bv_sb, "wo": wo_sb}
        NW = len(weights)
        const = {"ident": (ident_sb[:], ident), "spread": (spread_sb[:], spread)}
        if rel:
            const |= {"tab_h": (tab_h[:], w["tab_h"]), "tab_w": (tab_w[:], w["tab_w"])}
            for g in range(G):
                const[f"onehot{g}"] = (KK[:, g, :], w["onehot"])
        if window:
            const |= {"mask": (mask_sb[:], w["mask"]), "regs": (X[:, :, TOKENS:], w["regs"])}
        if rotary:
            const |= {"cos": (cos_sb[:], w["cos"]), "sin": (sin_sb[:], w["sin"]), "sign": (sign_sb[:], w["sign"])}

        consts_loaded = sem("consts_loaded")
        w_loaded = sem("w_loaded")
        w_scaled = sem("w_scaled")
        prepared = sem("prepared")
        x_loaded = sem("x_loaded")
        acc_loaded = sem("acc_loaded")
        acc_stored = sem("acc_stored")
        proj_done = sem("proj_done")
        q_out = sem("q_out")
        k_out = sem("k_out") if window else None
        moved = sem("moved") if rel else None
        rel_done = sem("rel_done") if rel else None
        rel_dve, rel_act = (sem("rel_dve"), sem("rel_act")) if rel else (None, None)
        vt_out = sem("vt_out")
        v_turned = sem("v_turned")
        v_placed = sem("v_placed")
        s_ready = sem("s_ready")
        max_done = sem("max_done")
        exp_done = sem("exp_done")
        turned = sem("turned")
        evac_dve, evac_act = sem("evac_dve"), sem("evac_act")
        pv_done = sem("pv_done")
        o_out = sem("o_out")
        sums_ready = sem("sums_ready")
        norm = sem("norm")
        y_ready = sem("y_ready")
        y_added = sem("y_added")
        mask_loaded = sem("mask_loaded") if rotary else None
        TURNS = 1 if window else 2
        PROJ = {"rel": 2, "window": 3, "rotary": 5}[kind]
        EVACS = TILES // 2 if window else TILES
        block = ctx.enter_context(nc.Block())

        @block.sync
        def _(sp):
            for dst, src in const.values():
                sp.dma_start(dst, src).then_inc(consts_loaded, 16)
            with sp.Fori(0, GROUPS) as hg:
                for n, dst in weights.items():
                    sp.dma_start(dst[:], w[n][hg]).then_inc(w_loaded, 16)
                if rotary:
                    for c in range(CHUNKS):
                        sp.dma_start(mask_sb[:, :, c, :], w["mask"][hg, c]).then_inc(mask_loaded, 16)
                with sp.Fori(0, IMAGES) as b:
                    u = hg * IMAGES + b
                    sp.dma_start(X[:, :, 0:TOKENS], xn[b]).then_inc(x_loaded, 16)
                    if rel:
                        sp.wait_ge(q_out, u + 1)
                        for g in range(G):
                            q_rows, k_rows = QK[DIM * g:DIM * g + DIM, :], QK[64 + DIM * g:64 + DIM * g + DIM, :]
                            sp.dma_start(QC[:, g, :], q_rows).then_inc(moved, 16)
                            sp.dma_start(KK[0:DIM, g, :], k_rows[:, 0:BANK]).then_inc(moved, 16)
                            sp.dma_start(KK[96:96 + DIM, g, :], k_rows[:, BANK:]).then_inc(moved, 16)
                    sp.wait_ge(proj_done, PROJ * u + PROJ)
                    sp.dma_start(ACC[:, :, 0:TOKENS], stream_in[b]).then_inc(acc_loaded, 16)
                    sp.wait_ge(y_added, 2 * u + 2)
                    sp.dma_start(stream_out[b], ACC[:, :, 0:TOKENS]).then_inc(acc_stored, 16)
                    sp.wait_ge(acc_stored, 16 * u + 16)
                    alone(sp)
            sp.wait_ge(acc_stored, 16 * GROUPS * IMAGES)

        @block.tensor
        def _(pe):
            def project(w_sb, rows, s):
                for t in range(2):
                    for k in range(2):
                        last = nc.tensor.matmul(S[0:rows, s, t, :], w_sb[:, k, :], X[:, k, t * BANK:(t + 1) * BANK],
                                                start=k == 0, stop=k == 1)
                return last

            def project_regs(w_sb, rows, s):
                for k in range(2):
                    last = nc.tensor.matmul(PT[0:rows, s, 0:P], w_sb[:, k, :], X[:, k, TOKENS:KTOK],
                                            start=k == 0, stop=k == 1)
                return last

            def turn_v(u):
                pe.wait_ge(vt_out, (2 if window else 1) * (u + 1))
                alone(pe)
                for j in range(CHUNKS):
                    last = nc.tensor.transpose(M[:, 64 * j:64 * j + 64], VT[0:G * DIM, P * j:P * j + P],
                                               ident_sb[0:G * DIM, 0:G * DIM])
                if window:
                    last = nc.tensor.transpose(PT[:, 0, 0:64], VT[0:G * DIM, TOKENS:KTOK],
                                               ident_sb[0:G * DIM, 0:G * DIM])
                last.then_inc(v_turned, 1)

            def scores(u, t):
                c, g = divmod(t, G)
                s, cols = t % 2, slice(P * c, P * c + P)
                if t >= 2:
                    if rel:
                        pe.wait_ge(exp_done, TILES * u + t - 1)
                    else:
                        pe.wait_ge(max_done, TILES * u + t - 1)
                if rel:
                    for h in range(2):
                        r = slice(64 * h, 64 * h + 64)
                        last = nc.tensor.matmul(S[:, s, h, :], QQ[r, g, cols], KK[r, g, :], start=True, stop=True)
                else:
                    r = slice(Q * g, Q * g + DIM)
                    if window:
                        k0 = P * min(max(c - 1, 0), CHUNKS - 3)
                        nc.tensor.matmul(S[:, s, 0, 0:3 * P], QQ[r, cols], KK[r, k0:k0 + 3 * P], start=True, stop=True)
                        last = nc.tensor.matmul(S[:, s, 0, 3 * P:], QQ[r, cols], KK[r, TOKENS:KTOK],
                                                start=True, stop=True)
                    else:
                        for h in range(2):
                            last = nc.tensor.matmul(S[:, s, h, :], QQ[r, cols], KK[r, h * BANK:(h + 1) * BANK],
                                                    start=True, stop=True)
                last.then_inc(s_ready, 1)

            def turn(u, t):
                pe.wait_ge(exp_done, TILES * u + t + 1)
                if t == 0:
                    pe.wait_ge(v_placed, (2 if window else 1) * (u + 1))
                if window:
                    if t >= 2:
                        pe.wait_ge(evac_act if t % 2 else evac_dve, EVACS * u + t // 2)
                    for j in range(4):
                        last = nc.tensor.transpose(PT[:, t % 2, P * j:P * j + P], PROB[:, t % 2, P * j:P * j + P],
                                                   ident_sb[:])
                    last.then_inc(turned, 1)
                    return
                for h, evac in ((0, evac_dve), (1, evac_act)):
                    if t:
                        pe.wait_ge(evac, TILES * u + t)
                    for j in range(4):
                        k = BANK * h + P * j
                        last = nc.tensor.transpose(PT[:, h, P * j:P * j + P], PROB[:, t % 2, k:k + P], ident_sb[:])
                    last.then_inc(turned, 1)

            def output(u, c):
                n = 2 * c + 2 if window else 4 * c + 4
                pe.wait_ge(evac_dve, EVACS * u + n)
                pe.wait_ge(evac_act, EVACS * u + n)
                if c == 4:
                    pe.wait_ge(o_out, 2 * u + 1)
                k0 = min(max(c - 1, 0), CHUNKS - 3)
                blocks = [(k0 + j, j) for j in range(3)] + [(CHUNKS, 3)] if window else [(j, j) for j in range(CHUNKS)]
                for i, (vj, j) in enumerate(blocks):
                    for g in range(G):
                        last = nc.tensor.matmul(O[Q * g:Q * g + VW, P * (c % 4):P * (c % 4) + P], V[:, vj, g, :],
                                                PTS[:, c % 2, g, P * j:P * j + P],
                                                start=i == 0, stop=i == len(blocks) - 1)
                last.then_inc(pv_done, 1)

            pe.wait_ge(consts_loaded, 16 * len(const))
            pe.wait_ge(prepared, 1)
            with pe.Fori(0, GROUPS) as hg:
                pe.wait_ge(w_loaded, 16 * NW * hg + 16 * NW)
                pe.wait_ge(w_scaled, hg + 1)
                alone(pe)
                with pe.Fori(0, IMAGES) as b:
                    u = hg * IMAGES + b
                    pe.wait_ge(x_loaded, 16 * u + 16)
                    if rel:
                        project(weights["wqk"], P, 0).then_inc(proj_done, 1)
                        project(wv_sb, G * DIM, 1).then_inc(proj_done, 1)
                        turn_v(u)
                        pe.wait_ge(moved, 16 * 3 * G * u + 16 * 3 * G)
                        alone(pe)
                        for r in range(4):
                            if r >= 2:
                                pe.wait_ge(rel_dve, 8 * u + 2 * r - 2)
                                pe.wait_ge(rel_act, 8 * u + 2 * r - 2)
                                alone(pe)
                            for il in range(8):
                                i, cols = 8 * r + il, slice((il % 4) * P, (il % 4) * P + P)
                                by_row, by_col = QC[:, :, SIDE * i:SIDE * i + SIDE], QC[:, :, i:TOKENS:SIDE]
                                table = tab_w[:, SIDE - 1 - i:2 * SIDE - 1 - i]
                                out = S[:, r % 2, il // 4, cols]
                                nc.tensor.matmul(out[0:Q, :], tab_h[:, 0, i, :], by_row, start=True, stop=True)
                                nc.tensor.matmul(out[Q:2 * Q, :], table, by_col, start=True, stop=True)
                                nc.tensor.matmul(out[2 * Q:3 * Q, :], table, by_col, start=True, stop=True)
                                last = nc.tensor.matmul(out[3 * Q:4 * Q, :], tab_h[:, 1, i, :], by_row,
                                                        start=True, stop=True)
                            last.then_inc(rel_done, 1)
                        pe.wait_ge(rel_dve, 8 * u + 8)
                        pe.wait_ge(rel_act, 8 * u + 8)
                    if window:
                        project(weights["wq"], P, 0).then_inc(proj_done, 1)
                        project(weights["wk"], P, 1)
                        project_regs(weights["wk"], P, 0).then_inc(proj_done, 1)
                        pe.wait_ge(q_out, u + 1)
                        project(wv_sb, G * DIM, 0)
                        project_regs(wv_sb, G * DIM, 1).then_inc(proj_done, 1)
                        pe.wait_ge(k_out, 2 * u + 2)
                        turn_v(u)
                    if rotary:
                        project(weights["wq"], P, 0).then_inc(proj_done, 1)
                        project(weights["wqr"], P, 1).then_inc(proj_done, 1)
                        pe.wait_ge(q_out, 6 * u + 1)
                        project(weights["wk"], P, 0).then_inc(proj_done, 1)
                        pe.wait_ge(q_out, 6 * u + 2)
                        project(weights["wkr"], P, 1).then_inc(proj_done, 1)
                        pe.wait_ge(q_out, 6 * u + 4)
                        project(wv_sb, G * DIM, 0).then_inc(proj_done, 1)
                        turn_v(u)
                        pe.wait_ge(q_out, 6 * u + 6)
                    scores(u, 0)
                    scores(u, 1)
                    for t in range(TILES):
                        if t + 2 < TILES:
                            scores(u, t + 2)
                        turn(u, t)
                        if t % 4 == 1 and t > 4:
                            output(u, t // 4 - 1)
                    output(u, CHUNKS - 1)
                    pe.wait_ge(o_out, 2 * u + 2)
                    for t in range(2):
                        last = nc.tensor.matmul(PT[:, t, :], spread_sb[:], OSB[:, t * BANK:(t + 1) * BANK],
                                                start=True, stop=True)
                    last.then_inc(sums_ready, 1)
                    pe.wait_ge(norm, 2 * u + 2)
                    for m in range(2):
                        for t in range(2):
                            last = nc.tensor.matmul(S[0:HALF, m, t, :], wo_sb[:, m * HALF:(m + 1) * HALF],
                                                    OSB[:, t * BANK:(t + 1) * BANK], start=True, stop=True)
                    last.then_inc(y_ready, 1)
                    pe.wait_ge(y_added, 2 * u + 2)
                    alone(pe)

        @block.vector
        def _(eng):
            nc.vector.memset(O[:], 0.0)
            if rotary:
                eng.wait_ge(consts_loaded, 16 * len(const))
                nc.vector.tensor_scalar(sin_sb[:], sin_sb[:], sign_sb[:, 0:1], None, ALU.mult)
            nc.vector.memset(V[:], 1.0).then_inc(prepared, 1)
            if window:
                eng.wait_ge(consts_loaded, 16 * len(const))
            with eng.Fori(0, GROUPS) as hg:
                eng.wait_ge(w_loaded, 16 * NW * hg + 16 * NW)
                if rel:
                    nc.vector.tensor_scalar(weights["wqk"][:, :, 64:], weights["wqk"][:, :, 64:], SCALE, None, ALU.mult)
                    nc.vector.tensor_scalar(weights["bqk"][64:, :], weights["bqk"][64:, :], SCALE, None,
                                            ALU.mult).then_inc(w_scaled, 1)
                else:
                    scaled = ["wk", "bk"] + (["wkr", "bkr"] if rotary else [])
                    for n in scaled:
                        last = nc.vector.tensor_scalar(weights[n][:], weights[n][:], SCALE, None, ALU.mult)
                    last.then_inc(w_scaled, 1)
                eng.wait_ge(w_scaled, hg + 1)
                alone(eng)
                if rotary:
                    eng.wait_ge(mask_loaded, 16 * CHUNKS * hg + 16 * CHUNKS)
                    alone(eng)
                with eng.Fori(0, IMAGES) as b:
                    u = hg * IMAGES + b
                    if rel:
                        eng.wait_ge(proj_done, PROJ * u + 1)
                        nc.vector.tensor_scalar(QK[:], slot(0), weights["bqk"][:, 0:1], None, ALU.add).then_inc(q_out, 1)
                        for r in range(4):
                            eng.wait_ge(rel_done, 4 * u + r + 1)
                            rows = S[:, r % 2, :, :].rearrange("p a (i h x) -> p (a i) h x", h=G, x=SIDE)
                            q = QQ[:].rearrange("p h (i x) -> p i h x", x=SIDE)
                            qt = QQ[:].rearrange("p h (x i) -> p i h x", i=SIDE)
                            nc.vector.tensor_copy(q[0:Q, 8 * r:8 * r + 8, :, :], rows[0:Q]).then_inc(rel_dve, 1)
                            nc.vector.tensor_copy(qt[Q:2 * Q, 8 * r:8 * r + 8, :, :], rows[Q:2 * Q]).then_inc(rel_dve, 1)
                    if window:
                        eng.wait_ge(proj_done, PROJ * u + 1)
                        nc.vector.tensor_scalar(QQ[:], slot(0), weights["bq"][:, 0:1], None, ALU.add).then_inc(q_out, 1)
                        eng.wait_ge(proj_done, PROJ * u + 3)
                        nc.vector.tensor_scalar(VT[:, 0:TOKENS], slot(0, G * DIM), bv_sb[:, 0:1], None,
                                                ALU.add).then_inc(vt_out, 1)
                        nc.vector.tensor_scalar(VT[:, TOKENS:], PT[0:G * DIM, 1, 0:P], bv_sb[:, 0:1], None,
                                                ALU.add).then_inc(vt_out, 1)
                    if rotary:
                        part = [PTS[:, 0, i, :] for i in range(4)]
                        for i, (n, table) in enumerate((("bq", cos_sb), ("bqr", sin_sb), ("bk", cos_sb), ("bkr", sin_sb))):
                            eng.wait_ge(proj_done, PROJ * u + i + 1)
                            nc.vector.scalar_tensor_tensor(out=part[i], in0=slot(i % 2), scalar=weights[n][:, 0:1],
                                                           in1=table[:], op0=ALU.add, op1=ALU.mult).then_inc(q_out, 1)
                        eng.wait_ge(q_out, 6 * u + 4)
                        nc.vector.tensor_tensor(QQ[:], part[0], part[1], ALU.add).then_inc(q_out, 1)
                        nc.vector.tensor_tensor(KK[:], part[2], part[3], ALU.add).then_inc(q_out, 1)

                    def row_max(t):
                        c, g = divmod(t, G)
                        eng.wait_ge(s_ready, TILES * u + t + 1)
                        if rel:
                            nc.vector.tensor_reduce(nmax[:, t % 4:t % 4 + 1], slot(t % 2), AX.X, ALU.max,
                                                    negate=True).then_inc(max_done, 1)
                            return
                        if t >= 2:
                            eng.wait_ge(turned, TURNS * (TILES * u + t - 1))
                        if window:
                            src, add = S[:, t % 2, 0, :], mask_sb[:, 0 if c == 0 else 2 if c == CHUNKS - 1 else 1, :]
                        else:
                            src, add = slot(t % 2), mask_sb[:, g, c, :]
                        alone(eng)
                        nc.vector.tensor_tensor_reduce(out=PROB[:, t % 2, :], in0=src, in1=add, scale=-1.0, scalar=BIG,
                                                       op0=ALU.add, op1=ALU.min,
                                                       accum_out=nmax[:, t % 4:t % 4 + 1]).then_inc(max_done, 1)

                    def evacuate(t):
                        if window and t % 2:
                            return
                        c, g = divmod(t, G)
                        eng.wait_ge(turned, TURNS * (TILES * u + t) + 1)
                        if c >= 2 and g == 0:
                            eng.wait_ge(pv_done, CHUNKS * u + c - 1)
                        nc.vector.tensor_copy(PTS[:, c % 2, g, 0:BANK], PT[:, (t % 2) if window else 0, :]).then_inc(evac_dve, 1)

                    row_max(0)
                    row_max(1)
                    for t in range(TILES):
                        if rel:
                            evacuate(t)
                            if t + 2 < TILES:
                                row_max(t + 2)
                        else:
                            evacuate(t)
                            if t + 2 < TILES:
                                row_max(t + 2)
                    eng.wait_ge(sums_ready, u + 1)
                    nc.vector.reciprocal(PTS[:, 0, 0:2, 0:BANK], PT[:]).then_inc(norm, 1)
                    eng.wait_ge(norm, 2 * u + 1)
                    nc.vector.tensor_tensor(OSB[:].rearrange("p (a b) -> p a b", a=2),
                                            OSB[:].rearrange("p (a b) -> p a b", a=2), PTS[:, 0, 0:2, 0:BANK],
                                            ALU.mult).then_inc(norm, 1)
                    eng.wait_ge(y_ready, u + 1)
                    eng.wait_ge(acc_loaded, 16 * u + 16)
                    for m in range(2):
                        nc.vector.tensor_tensor(ACC[:, m, 0:TOKENS], slot(m, HALF), ACC[:, m, 0:TOKENS],
                                                ALU.add).then_inc(y_added, 1)

        @block.scalar
        def _(act):
            act.wait_ge(prepared, 1)
            with act.Fori(0, GROUPS) as hg:
                act.wait_ge(w_loaded, 16 * NW * hg + 16 * NW)
                act.wait_ge(w_scaled, hg + 1)
                with act.Fori(0, IMAGES) as b:
                    u = hg * IMAGES + b
                    if window:
                        act.wait_ge(proj_done, PROJ * u + 2)
                        nc.scalar.activation(KK[:, 0:TOKENS], slot(1), ACT.Identity,
                                             bias=weights["bk"][:, 0:1]).then_inc(k_out, 1)
                        nc.scalar.activation(KK[:, TOKENS:], PT[:, 0, 0:P], ACT.Identity,
                                             bias=weights["bk"][:, 0:1]).then_inc(k_out, 1)
                    else:
                        act.wait_ge(proj_done, PROJ * u + PROJ)
                        nc.scalar.activation(VT[0:G * DIM, :], slot(1 if rel else 0, G * DIM), ACT.Identity,
                                             bias=bv_sb[:, 0:1]).then_inc(vt_out, 1)
                    act.wait_ge(v_turned, u + 1)
                    nc.scalar.copy(V[:, 0:CHUNKS, :, 0:DIM],
                                   M[:].rearrange("p (j h d) -> p j h d", h=G, d=DIM)).then_inc(v_placed, 1)
                    if window:
                        nc.scalar.copy(V[:, CHUNKS, :, 0:DIM],
                                       PT[:, 0, 0:64].rearrange("p (h d) -> p h d", d=DIM)).then_inc(v_placed, 1)
                    if rel:
                        for r in range(4):
                            act.wait_ge(rel_done, 4 * u + r + 1)
                            rows = S[:, r % 2, :, :].rearrange("p a (i h x) -> p (a i) h x", h=G, x=SIDE)
                            q = QQ[:].rearrange("p h (i x) -> p i h x", x=SIDE)
                            qt = QQ[:].rearrange("p h (x i) -> p i h x", i=SIDE)
                            nc.scalar.copy(qt[2 * Q:3 * Q, 8 * r:8 * r + 8, :, :], rows[2 * Q:3 * Q]).then_inc(rel_act, 1)
                            nc.scalar.copy(q[3 * Q:, 8 * r:8 * r + 8, :, :], rows[3 * Q:]).then_inc(rel_act, 1)

                    def exponential(t):
                        act.wait_ge(max_done, TILES * u + t + 1)
                        if rel and t >= 2:
                            act.wait_ge(turned, TURNS * (TILES * u + t - 1))
                        src = slot(t % 2) if rel else PROB[:, t % 2, :]
                        nc.scalar.activation(PROB[:, t % 2, :], src, ACT.Exp, bias=nmax[:, t % 4:t % 4 + 1],
                                             scale=1.0 if rel else -1.0).then_inc(exp_done, 1)

                    def evacuate(t):
                        if window and t % 2 == 0:
                            return
                        c, g = divmod(t, G)
                        act.wait_ge(turned, TURNS * (TILES * u + t + 1))
                        if c >= 2 and g == (1 if window else 0):
                            act.wait_ge(pv_done, CHUNKS * u + c - 1)
                        k0 = 0 if window else BANK
                        nc.scalar.copy(PTS[:, c % 2, g, k0:k0 + BANK], PT[:, 1, :]).then_inc(evac_act, 1)

                    def outputs(half):
                        act.wait_ge(pv_done, CHUNKS * u + 4 * half + 4)
                        nc.scalar.copy(OSB[:, half * BANK:(half + 1) * BANK], O[:]).then_inc(o_out, 1)

                    exponential(0)
                    for t in range(TILES):
                        if t + 1 < TILES:
                            exponential(t + 1)
                        evacuate(t)
                        if t == 18:
                            outputs(0)
                    outputs(1)


def program(nc, a, out):
    def scratch(n):
        return nc.dram_tensor(n, (IMAGES, HALF, 2, TOKENS), F32).ap()

    xn = scratch("xn_scratch")
    streams = [scratch(f"stream{i}") for i in range(3)] + [out]
    x = a["x"]
    sems = ExitStack()
    for i, kind in enumerate(("rel", "window", "rel", "rotary")):
        pre = f"L{i}_"
        w = {n[3:]: ap for n, ap in a.items() if n.startswith(pre)}
        lepe = {"wv": w["wv_all"], "bv": w["bv_all"], "lw": w["lw"], "lb": w["lb"], "wo": w["wo_all"]} if i == 3 else None
        normalise_block(nc, sems, f"n{i}", x, xn, streams[i], w["bo"], a["gavg"], lepe)
        attend_block(nc, sems, f"a{i}", kind, xn, streams[i], streams[i], w, a["ident"], a["spread"])
        x = streams[i]
    sems.close()


def _halves(w):
    return w.reshape(2, HALF, -1).transpose(1, 0, 2)


def _by_group(w):
    return _halves(w).reshape(HALF, 2, GROUPS, G * DIM).transpose(2, 0, 1, 3)


def _spread_heads(w):
    z = np.zeros(w.shape[:-1] + (G, Q), w.dtype)
    z[..., 0:DIM] = w.reshape(w.shape[:-1] + (G, DIM))
    return z.reshape(w.shape[:-1] + (P,))


def _turn_pairs(w):
    return w.reshape(w.shape[:-1] + (-1, 2))[..., ::-1].reshape(w.shape)


def _layouts(inp):
    f = np.float32
    a = {}
    a["x"] = inp["x"].reshape(IMAGES, TOKENS, 2, HALF).transpose(0, 3, 2, 1)
    a["ident"] = np.eye(P, dtype=f)
    a["spread"] = np.zeros((P, P), f)
    for g in range(G):
        a["spread"][Q * g + DIM, Q * g:Q * g + Q] = 1
    group = np.arange(HALF) // 6
    a["gavg"] = ((group[:, None] == group[None, :]) / 6.0).astype(f)

    qkv = {0: inp["L0_conv_w_qkv"], 1: inp["L1_conv_qkv_w"].T, 2: inp["L2_conv_qkv_w"].T,
           3: [inp[f"L3_conv_w{n}"].T for n in "qkv"]}
    bias = {0: inp["L0_conv_b_qkv"], 1: inp["L1_conv_qkv_b"], 2: inp["L2_conv_qkv_b"],
            3: [inp[f"L3_conv_b{n}"] for n in "qkv"]}
    wo = {0: inp["L0_conv_w_proj"], 1: inp["L1_conv_out_w"].T, 2: inp["L2_conv_proj_w"].T, 3: inp["L3_conv_wo"].T}
    bo = {0: inp["L0_conv_b_proj"], 1: inp["L1_conv_out_b"], 2: inp["L2_conv_proj_b"], 3: inp["L3_conv_bo"]}
    for i in range(4):
        if i == 3:
            (wq, wk, wv), (bq, bk, bv) = qkv[3], bias[3]
        else:
            wq, wk, wv = (qkv[i][:, n * CHANNELS:(n + 1) * CHANNELS] for n in range(3))
            bq, bk, bv = (bias[i][n * CHANNELS:(n + 1) * CHANNELS] for n in range(3))
        def by(b):
            return b.reshape(GROUPS, G * DIM)
        p = f"L{i}_"
        a[p + "wv"], a[p + "bv"] = _by_group(wv), by(bv)[:, :, None]
        a[p + "wo"] = _spread_heads(wo[i].T.reshape(CHANNELS, GROUPS, G * DIM).transpose(1, 0, 2)).transpose(0, 2, 1)
        a[p + "bo"] = bo[i].reshape(2, HALF).T
        if i in (0, 2):
            a[p + "wqk"] = np.concatenate([_by_group(wq), _by_group(wk)], axis=-1)
            a[p + "bqk"] = np.concatenate([by(bq), by(bk)], axis=-1)[:, :, None]
            rh = inp[f"L{i}_conv_rel_pos_h"][::-1].T
            rw = inp[f"L{i}_conv_rel_pos_w"][::-1].T
            tab = np.zeros((DIM, 2, SIDE, Q), f)
            for v in range(2):
                for row in range(SIDE):
                    tab[:, v, row, 0:DIM] = np.eye(DIM, dtype=f)
                    k = SIDE - 1 - row + DIM * v
                    tab[:, v, row, DIM:] = rh[:, k:k + DIM]
            a[p + "tab_h"], a[p + "tab_w"] = tab, rw
            key = np.arange(BANK)
            one = np.zeros((P, BANK), f)
            one[DIM + key // SIDE, key] = 1
            one[Q + key % SIDE, key] = 1
            one[2 * Q + key % SIDE, key] = 1
            one[3 * Q + DIM + key // SIDE, key] = 1
            a[p + "onehot"] = one
        else:
            for n, (wn, bn) in {"q": (wq, bq), "k": (wk, bk)}.items():
                a[p + "w" + n] = _spread_heads(_by_group(wn))
                a[p + "b" + n] = _spread_heads(by(bn))[:, :, None]
                if i == 3:
                    a[p + "w" + n + "r"] = _spread_heads(_by_group(_turn_pairs(wn)))
                    a[p + "b" + n + "r"] = _spread_heads(by(_turn_pairs(bn)))[:, :, None]
        if i == 1:
            regs = np.zeros((CHANNELS, P), f)
            regs[:, 0:REGS] = inp["L1_conv_registers"].T
            a[p + "regs"] = _halves(regs)
            mask = np.full((P, 3, KEYS_W), -1e30, f)
            for n, c, k0 in ((0, 0, 0), (1, 1, 0), (2, CHUNKS - 1, CHUNKS - 3)):
                q, k = P * c + np.arange(P), P * k0 + np.arange(3 * P)
                ok = np.ones((P, 3 * P), bool)
                for qi, ki in ((q // SIDE, k // SIDE), (q % SIDE, k % SIDE)):
                    start = np.clip(qi - WINDOW // 2, 0, SIDE - WINDOW)[:, None]
                    ok &= (ki[None, :] >= start) & (ki[None, :] < start + WINDOW)
                mask[:, n, 0:3 * P][ok] = 0
                mask[:, n, 3 * P:3 * P + REGS] = 0
            a[p + "mask"] = mask
        if i == 3:
            a[p + "wv_all"], a[p + "bv_all"] = _halves(wv), bv.reshape(2, HALF).T
            a[p + "wo_all"] = _halves(wo[3])
            a[p + "lw"] = inp["L3_conv_lepe_w"].reshape(TAPS * TAPS, 2, HALF).transpose(2, 1, 0)
            a[p + "lb"] = inp["L3_conv_lepe_b"].reshape(2, HALF).T
            for n in ("sin", "cos"):
                t = np.zeros((G, Q, TOKENS), f)
                t[:, 0:DIM] = inp[f"L3_conv_{n}"].reshape(TOKENS, DIM).T
                a[p + n] = t.reshape(P, TOKENS)
            a[p + "sign"] = np.where(np.arange(P) % 2, 1.0, -1.0).astype(f)[:, None]
            a[p + "mask"] = inp["L3_conv_mask"].reshape(GROUPS, G, CHUNKS, P, TOKENS).transpose(0, 2, 3, 1, 4)
    return {n: np.ascontiguousarray(v) for n, v in a.items()}


def kernel(**inputs):
    import concourse.bacc as _bacc
    from concourse.bass_utils import run_bass_kernel_spmd as _run

    arrays = _layouts({n: np.asarray(v) for n, v in inputs.items()})
    nc = _bacc.Bacc("TRN2", target_bir_lowering=False, num_devices=1)
    aps = {n: nc.dram_tensor(n, v.shape, mybir.dt.from_np(v.dtype), kind="ExternalInput").ap() for n, v in arrays.items()}
    out = nc.dram_tensor("out", (IMAGES, HALF, 2, TOKENS), F32, kind="ExternalOutput").ap()
    program(nc, aps, out)
    r = _run(nc, [arrays], core_ids=[0])
    y = r.results[0]["out"]
    return y.transpose(0, 3, 2, 1).reshape(IMAGES, SIDE, SIDE, CHANNELS)
```

```python
from contextlib import ExitStack

import numpy as np

import concourse.bass as bass
from concourse import mybir

ALU = mybir.AluOpType
ACT = mybir.ActivationFunctionType
AX = mybir.AxisListType
F32, BF16 = mybir.dt.float32, mybir.dt.bfloat16

P = 128
IMAGES, SIDE, CHANNELS, HEADS = 8, 32, 192, 12
TOKENS = SIDE * SIDE
DIM = CHANNELS // HEADS
GROUPS = 3
G = HEADS // GROUPS
HALF = CHANNELS // 2
CHUNKS = TOKENS // P
TILES = CHUNKS * G
Q = 32
BANK = 512
SCALE = float(DIM) ** -0.5
WINDOW, REGS = 7, 16
KEYS_W = 4 * P
BIG = 3.0e38
TAPS = 5
PAD = SIDE + TAPS - 1
GN_EPS = 1e-5
PAIRS = ((0, 0), (0, 1), (1, 0), (0, 2), (2, 0), (1, 1))
PARTS = 3


def alone(eng):
    eng.nop(nofuse=True)


def normalise_block(nc, sems, name, x_in, xn_out, stream_out, bias, gavg, lepe=None):
    with ExitStack() as ctx:
        def sb(n, shape):
            return ctx.enter_context(nc.sbuf_tensor(f"{name}_{n}", shape, F32))

        def sem(n):
            return sems.enter_context(nc.semaphore(f"{name}_{n}"))

        X = sb("x", [HALF, 2, TOKENS])
        XN = sb("xn", [HALF, 2, TOKENS])
        ST = sb("stream", [HALF, 2, TOKENS])
        bias_sb = sb("bias", [HALF, 2])
        gavg_sb = sb("gavg", [HALF, HALF])
        stats = sb("stats", [HALF, 2, 2, 6])
        mv = sb("mv", [HALF, 2, 2])
        sq = sb("sq", [HALF, 2])
        me = sb("me", [HALF, 2, 2])
        gm = sb("gm", [HALF, 2, 2])
        gsq = sb("gsq", [HALF, 2])
        var = sb("var", [HALF, 2])
        power = sb("power", [HALF, 2])
        rstd = sb("rstd", [HALF, 2])
        ps_g = ctx.enter_context(nc.psum_tensor(f"{name}_psg", [P, BANK], F32))
        loaded_c = sem("loaded_c")
        loaded_x = sem("loaded_x")
        stored_xn = sem("stored_xn")
        stored_st = sem("stored_st")
        power_set = sem("power_set")
        dve = sem("dve")
        averaged = sem("averaged")
        exponent_set = sem("exponent_set")
        powered = sem("powered")
        xn_ready = sem("xn_ready")
        st_ready = sem("st_ready")
        if lepe:
            VP = sb("vpad", [HALF, 2, PAD, PAD])
            CV = sb("conv", [HALF, 2, TOKENS])
            wv_sb = sb("wv", [HALF, 2, CHANNELS])
            bv_sb = sb("bv", [HALF, 2])
            lw_sb = sb("lw", [HALF, 2, TAPS * TAPS])
            lb_sb = sb("lb", [HALF, 2])
            wo_sb = sb("wo", [HALF, 2, CHANNELS])
            ps_v = ctx.enter_context(nc.psum_tensor(f"{name}_psv", [P, 4, BANK], F32))
            v_ready = sem("v_ready")
            v_padded = sem("v_padded")
            pad_set = sem("pad_set")
            taps = sem("taps")
            o_ready = sem("o_ready")
            st_added = sem("st_added")
        consts = 2 + (5 if lepe else 0)
        DVE_STEPS = 11
        NT = 2 * TAPS * TAPS
        block = ctx.enter_context(nc.Block())

        @block.sync
        def _(sp):
            sp.dma_start(bias_sb[:], bias).then_inc(loaded_c, 16)
            sp.dma_start(gavg_sb[:], gavg).then_inc(loaded_c, 16)
            if lepe:
                for dst, src in ((wv_sb, "wv"), (bv_sb, "bv"), (lw_sb, "lw"), (lb_sb, "lb"), (wo_sb, "wo")):
                    sp.dma_start(dst[:], lepe[src]).then_inc(loaded_c, 16)
            with sp.Fori(0, IMAGES) as b:
                sp.dma_start(X[:], x_in[b]).then_inc(loaded_x, 16)
                sp.wait_ge(xn_ready, 2 * b + 2)
                sp.dma_start(xn_out[b], XN[:]).then_inc(stored_xn, 16)
                sp.wait_ge(st_ready, b + 1)
                if lepe:
                    sp.wait_ge(st_added, 2 * b + 2)
                sp.dma_start(stream_out[b], ST[:]).then_inc(stored_st, 16)
            sp.wait_ge(stored_xn, 16 * IMAGES)
            sp.wait_ge(stored_st, 16 * IMAGES)

        @block.vector
        def _(eng):
            if lepe:
                nc.vector.memset(VP[:], 0.0).then_inc(pad_set, 1)
            with eng.Fori(0, IMAGES) as b:
                base = b * DVE_STEPS
                eng.wait_ge(loaded_x, 16 * b + 16)
                for m in range(2):
                    for h in range(2):
                        nc.vector.bn_stats(stats[:, m, h, :], X[:, m, h * BANK:(h + 1) * BANK]).then_inc(dve, 1)
                eng.wait_ge(dve, base + 4)
                alone(eng)
                for m in range(2):
                    nc.vector.bn_aggr(mv[:, m, :], stats[:, m, :, :].rearrange("p a b -> p (a b)")).then_inc(dve, 1)
                eng.wait_ge(dve, base + 6)
                nc.vector.tensor_tensor(sq[:], mv[:, :, 0], mv[:, :, 0], ALU.mult).then_inc(dve, 1)
                nc.vector.tensor_copy(me[:, :, 0], mv[:, :, 0]).then_inc(dve, 1)
                eng.wait_ge(dve, base + 8)
                nc.vector.tensor_tensor(me[:, :, 1], sq[:], mv[:, :, 1], ALU.add).then_inc(dve, 1)
                eng.wait_ge(averaged, b + 1)
                nc.vector.tensor_copy(gm[:], ps_g[0:HALF, 0:4].rearrange("p (a b) -> p a b", a=2)).then_inc(dve, 1)
                eng.wait_ge(dve, base + 10)
                nc.vector.tensor_tensor(gsq[:], gm[:, :, 0], gm[:, :, 0], ALU.mult).then_inc(dve, 1)
                eng.wait_ge(dve, base + 11)
                nc.vector.scalar_tensor_tensor(out=var[:], in0=gm[:, :, 1], scalar=GN_EPS, in1=gsq[:],
                                               op0=ALU.add, op1=ALU.subtract).then_inc(power_set, 1)
                eng.wait_ge(powered, b + 1)
                for m in range(2):
                    nc.vector.tensor_scalar(XN[:, m, :], X[:, m, :], gm[:, m, 0:1], rstd[:, m:m + 1],
                                            ALU.subtract, ALU.mult).then_inc(xn_ready, 1)
                if lepe:
                    eng.wait_ge(v_padded, 2 * b + 2)
                    for k in range(TAPS * TAPS):
                        dy, dx = divmod(k, TAPS)
                        for m in range(2):
                            n = NT * b + 2 * k + m
                            src = VP[:, m, dy:dy + SIDE, dx:dx + SIDE]
                            dst = CV[:, m, :].rearrange("p (a b) -> p a b", a=SIDE)
                            if k == 0:
                                ins = nc.vector.tensor_scalar(dst, src, lw_sb[:, m, 0:1], lb_sb[:, m:m + 1],
                                                              ALU.mult, ALU.add)
                            else:
                                eng.wait_ge(taps, n - 1)
                                ins = nc.vector.scalar_tensor_tensor(out=dst, in0=src, scalar=lw_sb[:, m, k:k + 1],
                                                                     in1=dst, op0=ALU.mult, op1=ALU.add)
                            ins.then_inc(taps, 1)
                    eng.wait_ge(o_ready, b + 1)
                    eng.wait_ge(st_ready, b + 1)
                    for m in range(2):
                        nc.vector.tensor_tensor(ST[:, m, :], ps_v[0:HALF, 2 * m:2 * m + 2, :].rearrange("p a b -> p (a b)"),
                                                ST[:, m, :], ALU.add).then_inc(st_added, 1)
                eng.wait_ge(stored_xn, 16 * b + 16)
                alone(eng)

        @block.tensor
        def _(pe):
            pe.wait_ge(loaded_c, 16 * consts)
            with pe.Fori(0, IMAGES) as b:
                pe.wait_ge(dve, b * DVE_STEPS + 9)
                nc.tensor.matmul(ps_g[0:HALF, 0:4], gavg_sb[:], me[:].rearrange("p a b -> p (a b)"),
                                 start=True, stop=True).then_inc(averaged, 1)
                if lepe:
                    pe.wait_ge(xn_ready, 2 * b + 2)
                    for m in range(2):
                        for t in range(2):
                            for k in range(2):
                                last = nc.tensor.matmul(ps_v[0:HALF, 2 * m + t, :], wv_sb[:, k, m * HALF:(m + 1) * HALF],
                                                        XN[:, k, t * BANK:(t + 1) * BANK], start=k == 0, stop=k == 1)
                    last.then_inc(v_ready, 1)
                    pe.wait_ge(taps, NT * b + NT)
                    pe.wait_ge(v_padded, 2 * b + 2)
                    for m in range(2):
                        for t in range(2):
                            for k in range(2):
                                last = nc.tensor.matmul(ps_v[0:HALF, 2 * m + t, :], wo_sb[:, k, m * HALF:(m + 1) * HALF],
                                                        CV[:, k, t * BANK:(t + 1) * BANK], start=k == 0, stop=k == 1)
                    last.then_inc(o_ready, 1)
                    pe.wait_ge(st_added, 2 * b + 2)
                    alone(pe)

        @block.scalar
        def _(act):
            act.wait_ge(loaded_c, 16 * consts)
            if lepe:
                act.wait_ge(pad_set, 1)
            with act.Fori(0, IMAGES) as b:
                act.wait_ge(loaded_x, 16 * b + 16)
                nc.scalar.activation(ST[:, 0, :], X[:, 0, :], ACT.Identity, bias=bias_sb[:, 0:1])
                nc.scalar.activation(ST[:, 1, :], X[:, 1, :], ACT.Identity, bias=bias_sb[:, 1:2]).then_inc(st_ready, 1)
                if lepe:
                    act.wait_ge(v_ready, b + 1)
                    for m in range(2):
                        nc.scalar.activation(VP[:, m, 2:2 + SIDE, 2:2 + SIDE],
                                             ps_v[0:HALF, 2 * m:2 * m + 2, :].rearrange("p a (y x) -> p (a y) x", x=SIDE),
                                             ACT.Identity, bias=bv_sb[:, m:m + 1]).then_inc(v_padded, 1)
                act.wait_ge(stored_st, 16 * b + 16)
                alone(act)

        @block.gpsimd
        def _(pool):
            nc.gpsimd.memset(power[:], -0.5).then_inc(exponent_set, 1)
            pool.wait_ge(exponent_set, 1)
            with pool.Fori(0, IMAGES) as b:
                pool.wait_ge(power_set, b + 1)
                nc.gpsimd.tensor_tensor(rstd[:], var[:], power[:], ALU.pow).then_inc(powered, 1)


def need(eng, sem, value, solo=False):
    if isinstance(value, int) and value <= 0:
        return
    eng.wait_ge(sem, value)
    if solo:
        alone(eng)


def attend_block(nc, sems, name, kind, xn, stream, w, ident):
    rel, window, rotary = kind == "rel", kind == "window", kind == "rotary"
    KTOK = TOKENS + (P if window else 0)
    VC = KTOK // P
    KEYS = KEYS_W if window else TOKENS
    SLOTS = 4 if window else 2
    PROBS = 2 if rotary else 4
    PTSLOTS = 1 if rotary else 2
    UNITS = GROUPS * IMAGES
    YS = 1 if rotary else 2
    LAG = 0 if rotary else 1
    WIDTHS = [BANK, BANK] + ([P] if window else [])
    PIECES = len(WIDTHS)
    STARTS = [BANK * i for i in range(PIECES)]
    with ExitStack() as ctx:
        def sb(n, shape, dt=F32):
            return ctx.enter_context(nc.sbuf_tensor(f"{name}_{n}", shape, dt))

        def sem(n):
            return sems.enter_context(nc.semaphore(f"{name}_{n}"))

        S = ctx.enter_context(nc.psum_tensor(f"{name}_S", [P, SLOTS, KEYS], F32))
        PT = ctx.enter_context(nc.psum_tensor(f"{name}_PT", [P, 2, BANK], F32))
        O = ctx.enter_context(nc.psum_tensor(f"{name}_O", [P, BANK], F32))
        M = ctx.enter_context(nc.psum_tensor(f"{name}_M", [P, BANK], F32))

        ident_sb = sb("ident", [P, P])
        wo_sb = sb("wo", [P, CHANNELS])
        wv_sb = sb("wv", [HALF, 2, G * DIM])
        bv_sb = sb("bv", [G * DIM, 1])
        XTOK = BANK if rotary else KTOK
        X = sb("X", [HALF, 2, XTOK])
        PTS = sb("PTS", [P, PTSLOTS, G, KEYS])
        OSB = sb("OSB", [P, BANK])
        Y = sb("Y", [HALF, YS, BANK])
        VT = sb("VT", [G * DIM, BANK])
        V = sb("V", [P, 2, VC, G, DIM])
        PROB = sb("PROB", [P, PROBS, KEYS])
        nmax = sb("nmax", [P, 4])
        sums = sb("sums", [P, TILES])
        inverse = sb("inverse", [P, TILES // 2])
        inverse_wide = sb("inverse_wide", [P, TILES // 2, Q])
        if rel:
            QQ = sb("QQ", [3 * Q, 2, G, TOKENS])
            KK = sb("KK", [3 * Q, 2, G, 2, BANK])
            QK = sb("QK", [P, TOKENS])
            QC = sb("QC", [DIM, G, TOKENS])
            tab_h = sb("tab_h", [DIM, 2, SIDE, Q])
            tab_w = sb("tab_w", [DIM, 2 * SIDE - 1])
            weights = {"wqk": sb("wqk", [HALF, 2, P]), "bqk": sb("bqk", [P, 1])}
            scaled = [(weights["wqk"][:, :, 64:]), (weights["bqk"][64:, :])]
        else:
            QQ = sb("QQ", [DIM * len(PAIRS), G, TOKENS], BF16)
            KK = sb("KK", [DIM * len(PAIRS), 2, G, KTOK], BF16)
            whole = sb("whole", [P, BANK])
            split_parts = sb("split_parts", [P, PARTS, BANK], BF16)
            parts = nc.dram_tensor(f"{name}_parts", (2, PARTS, P, KTOK), BF16).ap()
            weights = {}
            for n in ["qk"] + (["qkr"] if rotary else []):
                weights["w" + n] = sb("w" + n, [HALF, 2, P])
                weights["b" + n] = sb("b" + n, [P, 1])
            scaled = [(t[:, :, 64:] if n[0] == "w" else t[64:, :]) for n, t in weights.items()]
        if window:
            mask_sb = sb("mask", [P, 3, KEYS_W])
        if rotary:
            mask_sb = sb("mask", [P, G, CHUNKS, TOKENS])
            cos_sb = sb("cos", [P, BANK])
            sin_sb = sb("sin", [P, BANK])
            sign_sb = sb("sign", [P, 1])
        weights |= {"wv": wv_sb, "bv": bv_sb}
        NW = len(weights)
        const = {"ident": (ident_sb[:], ident)}
        if rel:
            const |= {"tab_h": (tab_h[:], w["tab_h"]), "tab_w": (tab_w[:], w["tab_w"])}
            for g in range(G):
                for par in range(2):
                    const[f"onehot{g}{par}"] = (KK[:, par, g, :, :], w["onehot"])
        if window:
            const |= {"mask": (mask_sb[:], w["mask"]), "regs": (X[:, :, TOKENS:], w["regs"])}
        if rotary:
            const |= {"sign": (sign_sb[:], w["sign"])}

        consts_loaded = sem("consts_loaded")
        loaded = sem("loaded")
        w_scaled = sem("w_scaled")
        loaded_more = sem("loaded_more") if rotary else None
        prepared = sem("prepared")
        moved = sem("moved") if rel else None
        if not rel:
            split = sem("split")
            parts_stored = sem("parts_stored")
            k_loaded = sem("k_loaded")
            q_loaded = [sem(f"q_loaded{h}") for h in range(2)]
        SPLIT_STEPS = 4
        prep_ready = sem("prep_ready")
        prep_dve, prep_act = sem("prep_dve"), sem("prep_act")
        tail_ready = sem("tail_ready")
        tail_dve, tail_act = sem("tail_dve"), sem("tail_act")
        s_ready = sem("s_ready")
        max_done = sem("max_done")
        exp_done = sem("exp_done")
        turned = sem("turned")
        evac_dve, evac_act = sem("evac_dve"), sem("evac_act")
        pv_done = sem("pv_done")
        o_out = sem("o_out")
        wo_loaded = sem("wo_loaded")
        y_stored = [sem(f"y_stored{s}") for s in range(YS)]
        inverted = sem("inverted")
        MASKS = 16 * CHUNKS // 2
        mask_loaded = [sem(f"mask_loaded{h}") for h in range(2)] if rotary else None
        LOADS = NW + (3 if rotary else 1)
        TURNS = 1 if window else 2
        EVACS = TILES // 2 if window else TILES
        read_done = exp_done if rel else max_done

        jobs = []

        def job(step, pe, dve=(), act=()):
            jobs.append((step, pe, list(dve), list(act)))

        def project(w_sb, rows, half):
            def run(n, par):
                cols = slice(STARTS[half], STARTS[half] + WIDTHS[half])
                if rotary:
                    cols = slice(0, BANK)
                    if half == 1:
                        nc.tensor.wait_ge(loaded_more, 16 * 3 * (n + 1))
                        alone(nc.tensor)
                for k in range(2):
                    last = nc.tensor.matmul(M[0:rows, 0:cols.stop - cols.start], w_sb[:, k, :], X[:, k, cols],
                                            start=k == 0, stop=k == 1)
                return last
            return run

        def v_out(half):
            width = BANK if half < 2 else P
            return lambda par: nc.scalar.activation(VT[:, 0:width], M[0:G * DIM, 0:width], ACT.Identity, bias=bv_sb[:, 0:1])

        def turn_v(half):
            blocks = 4 if half < 2 else 1

            def run(n, par):
                for j in range(blocks):
                    last = nc.tensor.transpose(M[:, 64 * j:64 * j + 64], VT[:, P * j:P * j + P],
                                               ident_sb[0:G * DIM, 0:G * DIM])
                return last

            def place(par):
                return nc.scalar.copy(V[:, par, 4 * half:4 * half + blocks, :, :],
                                      M[:, 0:64 * blocks].rearrange("p (j h d) -> p j h d", h=G, d=DIM))
            return run, place

        def add_v_jobs(step, halves):
            for i, half in enumerate(halves):
                job(step + 2 * i, project(wv_sb, G * DIM, half), act=[v_out(half)])
                run, place = turn_v(half)
                job(step + 2 * i + 1, run, act=[place])

        if rel:
            for half in range(2):
                job(7 + half, project(weights["wqk"], P, half), dve=[
                    lambda par, half=half: nc.vector.tensor_scalar(
                        QK[:, half * BANK:(half + 1) * BANK], M[:], weights["bqk"][:, 0:1], None, ALU.add)])
            add_v_jobs(9, range(2))

            def relative(r):
                def run(n, par):
                    if r == 0:
                        need(nc.tensor, moved, 16 * 3 * G * (n + 1))
                    alone(nc.tensor)
                    for il in range(4):
                        i, out = 4 * r + il, M[:, il * P:il * P + P]
                        by_row, by_col = QC[:, :, SIDE * i:SIDE * i + SIDE], QC[:, :, i:TOKENS:SIDE]
                        table = tab_w[:, SIDE - 1 - i:2 * SIDE - 1 - i]
                        nc.tensor.matmul(out[0:Q, :], tab_h[:, 0, i, :], by_row, start=True, stop=True)
                        nc.tensor.matmul(out[Q:2 * Q, :], table, by_col, start=True, stop=True)
                        last = nc.tensor.matmul(out[2 * Q:3 * Q, :], tab_h[:, 1, i, :], by_row, start=True, stop=True)
                    return last

                def put(copy, quadrant):
                    def run(par):
                        rows = slice(Q * quadrant, Q * quadrant + Q)
                        src = M[rows].rearrange("p (i h x) -> p i h x", h=G, x=SIDE)
                        order = "p h (x i) -> p i h x" if quadrant == 1 else "p h (i x) -> p i h x"
                        dst = QQ[rows, par].rearrange(order, **({"i": SIDE} if quadrant == 1 else {"x": SIDE}))
                        return copy(dst[:, 4 * r:4 * r + 4, :, :], src)
                    return run
                job(13 + r, run, dve=[put(nc.vector.tensor_copy, 0), put(nc.vector.tensor_copy, 1)],
                    act=[put(nc.scalar.copy, 2)])
            for r in range(8):
                relative(r)
        if not rel:
            def free_whole(n, piece):
                need(nc.vector, split, SPLIT_STEPS * (PIECES * n + piece), solo=True)
        if window:
            whole_made = []
            for piece, step in enumerate((7, 11, 14)):
                width = WIDTHS[piece]
                whole_made.append(len(jobs))
                job(step, project(weights["wqk"], P, piece), dve=[
                    ("free", piece),
                    lambda par, width=width: nc.vector.tensor_scalar(
                        whole[:, 0:width], M[:, 0:width], weights["bqk"][:, 0:1], None, ALU.add)])
                add_v_jobs(step + 1, [piece]) if piece < 2 else add_v_jobs(15, [piece])
        if rotary:
            whole_made = []
            for piece, step in enumerate((7, 15)):
                job(step, project(weights["wqk"], P, piece), dve=[
                    ("free", piece),
                    lambda par: nc.vector.scalar_tensor_tensor(
                        out=whole[:], in0=M[:], scalar=weights["bqk"][:, 0:1], in1=cos_sb[:],
                        op0=ALU.add, op1=ALU.mult)])
                whole_made.append(len(jobs))
                job(step + 1, project(weights["wqkr"], P, piece), dve=[
                    lambda par: nc.vector.scalar_tensor_tensor(
                        out=M[:], in0=M[:], scalar=weights["bqkr"][:, 0:1], in1=sin_sb[:],
                        op0=ALU.add, op1=ALU.mult),
                    "wait",
                    lambda par: nc.vector.scalar_tensor_tensor(
                        out=whole[:], in0=M[:], scalar=sign_sb[:, 0:1], in1=whole[:],
                        op0=ALU.mult, op1=ALU.add)])
                add_v_jobs(step + 2, [piece])
        NJ = len(jobs)
        count_dve = [sum(callable(f) for f in j[2]) for j in jobs]
        count_act = [len(j[3]) for j in jobs]
        PD, PA = sum(count_dve), sum(count_act)
        job_at = {j[0]: i for i, j in enumerate(jobs)}
        assert len(job_at) == NJ

        TAIL_AT = {22: (0, 0), 24: (0, 1), 26: (0, 2)}
        TAIL_AFTER = {3: (1, 0), 4: (1, 1), 6: (1, 2)}

        def prep_out(eng, n, j):
            need(eng, prep_dve, n * PD + sum(count_dve[:j + 1]))
            need(eng, prep_act, n * PA + sum(count_act[:j + 1]), solo=True)

        def tail_out(eng, n, half, which):
            if which == 0:
                need(eng, tail_dve, 4 * n + 2 * half + 2, solo=True)
            else:
                need(eng, tail_act, 4 * n + 2 * half + which, solo=True)

        block = ctx.enter_context(nc.Block())

        @block.sync
        def _(sp):
            for dst, src in const.values():
                sp.dma_start(dst, src).then_inc(consts_loaded, 16)

            def load_x(b, half, done):
                if not rotary:
                    sp.dma_start(X[:, :, 0:TOKENS], xn[b]).then_inc(done, 16)
                    return
                cols = slice(half * BANK, (half + 1) * BANK)
                sp.dma_start(X[:], xn[b][:, :, cols]).then_inc(done, 16)
                sp.dma_start(cos_sb[:], w["cos"][:, cols]).then_inc(done, 16)
                sp.dma_start(sin_sb[:], w["sin"][:, cols]).then_inc(done, 16)

            for hg in range(GROUPS):
                def load(hg, b, par, first=False):
                    n = hg * IMAGES + b
                    for nm, dst in weights.items():
                        sp.dma_start(dst[:], w[nm][hg]).then_inc(loaded, 16)
                    load_x(b, 0, loaded)
                    if rel:
                        sp.wait_ge(prep_dve, PD * n + 2)
                        alone(sp)
                        for g in range(G):
                            q_rows, k_rows = QK[DIM * g:DIM * g + DIM, :], QK[64 + DIM * g:64 + DIM * g + DIM, :]
                            sp.dma_start(QC[:, g, :], q_rows).then_inc(moved, 16)
                            sp.dma_start(KK[0:DIM, par, g, 0, :], k_rows[:, 0:BANK]).then_inc(moved, 16)
                            sp.dma_start(KK[2 * Q:2 * Q + DIM, par, g, 1, :], k_rows[:, BANK:]).then_inc(moved, 16)
                    else:
                        for piece in range(PIECES):
                            if rotary and piece == 1:
                                sp.wait_ge(prep_ready, NJ * n + NJ // 2)
                                alone(sp)
                                load_x(b, 1, loaded_more)
                            cols = slice(STARTS[piece], STARTS[piece] + WIDTHS[piece])
                            sp.wait_ge(split, SPLIT_STEPS * (PIECES * n + piece + 1))
                            alone(sp)
                            sp.dma_start(parts[par, :, :, cols].rearrange("s r t -> r s t"),
                                         split_parts[:, :, 0:WIDTHS[piece]]).then_inc(parts_stored, 16)
                        sp.wait_ge(parts_stored, 16 * PIECES * (n + 1))
                        alone(sp)
                        for i, (_, part) in enumerate(PAIRS):
                            sp.dma_start(KK[DIM * i:DIM * i + DIM, par], parts[par, part, G * DIM:, :].rearrange(
                                "(g c) t -> c g t", c=DIM)).then_inc(k_loaded, 16)
                        for half in range(2):
                            cols = slice(half * BANK, (half + 1) * BANK)
                            need(sp, s_ready, TILES * (n - 1) + TILES // 2 * (half + 1), solo=True)
                            for i, (part, _) in enumerate(PAIRS):
                                sp.dma_start(QQ[DIM * i:DIM * i + DIM, :, cols],
                                             parts[par, part, 0:G * DIM, cols].rearrange("(g c) t -> c g t", c=DIM)
                                             ).then_inc(q_loaded[half], 16)
                            if rotary and first:
                                for c in range(half * CHUNKS // 2, (half + 1) * CHUNKS // 2):
                                    need(sp, max_done, TILES * (n - 1) + G * (c + 1))
                                    sp.dma_start(mask_sb[:, :, c, :], w["mask"][hg, c]).then_inc(mask_loaded[half], 16)
                            elif rotary:
                                sp.wait_ge(mask_loaded[half], MASKS * n)
                                sp.sem_inc(mask_loaded[half], MASKS)
                    sp.wait_ge(prep_ready, NJ * n + NJ)
                    alone(sp)

                load(hg, 0, 0, first=True)
                load(hg, 1, 1)
                with sp.Fori(1, IMAGES // 2) as p:
                    load(hg, 2 * p, 0)
                    load(hg, 2 * p + 1, 1)

        @block.gpsimd
        def _(pool):
            def split_unit(n):
                for piece in range(PIECES):
                    width = WIDTHS[piece]
                    rest, hi, mid, lo = (whole[:, 0:width], *(split_parts[:, i, 0:width] for i in range(PARTS)))
                    base = SPLIT_STEPS * (PIECES * n + piece)
                    need(pool, parts_stored, 16 * (PIECES * n + piece), solo=True)
                    pool.wait_ge(prep_dve, PD * n + sum(count_dve[:whole_made[piece] + 1]))
                    alone(pool)
                    nc.gpsimd.tensor_copy(hi, rest).then_inc(split, 1)
                    pool.wait_ge(split, base + 1)
                    alone(pool)
                    nc.gpsimd.tensor_tensor(rest, rest, hi, ALU.subtract).then_inc(split, 1)
                    pool.wait_ge(split, base + 2)
                    alone(pool)
                    nc.gpsimd.tensor_copy(mid, rest).then_inc(split, 1)
                    pool.wait_ge(split, base + 3)
                    alone(pool)
                    nc.gpsimd.tensor_tensor(lo, rest, mid, ALU.subtract).then_inc(split, 1)

            def store_outputs(hg, b):
                u = hg * IMAGES + b
                pool.dma_start(wo_sb[:], w["wo"][hg]).then_inc(wo_loaded, 16)
                for k in range(4):
                    half, m = divmod(k, 2)
                    pool.wait_ge(tail_act, 4 * u + k + 1)
                    alone(pool)
                    pool.dma_start(stream[b][:, m, half * BANK:(half + 1) * BANK], Y[:, k % YS, :],
                                   accum_op=ALU.add).then_inc(y_stored[k % YS], 16)
                for done in y_stored:
                    pool.wait_ge(done, 64 // YS * (u + 1))
                alone(pool)

            if not rel:
                split_unit(0)
                split_unit(1)
            for hg in range(GROUPS):
                last = hg == GROUPS - 1
                with pool.Fori(0, IMAGES - 2 if last else IMAGES) as b:
                    store_outputs(hg, b)
                    if not rel:
                        split_unit(hg * IMAGES + b + 2)
                if last:
                    store_outputs(hg, IMAGES - 2)
                    store_outputs(hg, IMAGES - 1)

        def pairs(eng, prologue, body, epilogue):
            prologue()
            body(0, 0, True, False)
            body(1, 1, False, False)
            with eng.Fori(1, UNITS // 2 - 1) as p:
                body(2 * p, 0, False, False)
                body(2 * p + 1, 1, False, False)
            body(UNITS - 2, 0, False, False)
            body(UNITS - 1, 1, False, True)
            epilogue()

        @block.tensor
        def _(pe):
            def scores(u, par, tiles):
                todo = []
                need(pe, read_done, TILES * u + tiles[-1] - SLOTS + 1)
                for t in tiles:
                    c, g = divmod(t, G)
                    s, cols = t % SLOTS, slice(P * c, P * c + P)
                    if rel:
                        todo.append([(S[:, s, h * BANK:(h + 1) * BANK], QQ[:, par, g, cols], KK[:, par, g, h, :])
                                     for h in range(2)])
                    elif window:
                        k0 = P * min(max(c - 1, 0), CHUNKS - 3)
                        todo.append([(S[:, s, 0:3 * P], QQ[:, g, cols], KK[:, par, g, k0:k0 + 3 * P]),
                                     (S[:, s, 3 * P:], QQ[:, g, cols], KK[:, par, g, TOKENS:])])
                    else:
                        todo.append([(S[:, s, h * BANK:(h + 1) * BANK], QQ[:, g, cols],
                                      KK[:, par, g, h * BANK:(h + 1) * BANK]) for h in range(2)])
                    if not rel and t == TILES // 2:
                        pe.wait_ge(q_loaded[1], 16 * len(PAIRS) * (u + 1))
                alone(pe)
                for one in todo:
                    for i in range(2):
                        last = nc.tensor.matmul(*one[i], start=True, stop=True)
                    last.then_inc(s_ready, 1)

            def turn(u, t):
                T = TILES * u + t
                pe.wait_ge(exp_done, T + 1)
                for h in range(TURNS):
                    bank = t % 2 if window else h
                    if window:
                        need(pe, evac_act if t % 2 else evac_dve, EVACS * u + t // 2)
                    else:
                        need(pe, evac_act if h else evac_dve, T)
                    alone(pe)
                    for j in range(4):
                        k = BANK * h + P * j
                        last = nc.tensor.transpose(PT[:, bank, P * j:P * j + P], PROB[:, t % PROBS, k:k + P], ident_sb[:])
                    last.then_inc(turned, 1)

            def output(u, par, c):
                n = 2 * c + 2 if window else 4 * c + 4
                pe.wait_ge(evac_dve, EVACS * u + n)
                pe.wait_ge(evac_act, EVACS * u + n)
                if c % 4 == 0:
                    need(pe, o_out, 2 * u + c // 4)
                alone(pe)
                k0 = min(max(c - 1, 0), CHUNKS - 3)
                blocks = [(k0 + j, j) for j in range(3)] + [(CHUNKS, 3)] if window else [(j, j) for j in range(CHUNKS)]
                for i, (vj, j) in enumerate(blocks):
                    for g in range(G):
                        last = nc.tensor.matmul(O[Q * g:Q * g + DIM, P * (c % 4):P * (c % 4) + P], V[:, par, vj, g, :],
                                                PTS[:, c % PTSLOTS, g, P * j:P * j + P],
                                                start=i == 0, stop=i == len(blocks) - 1)
                last.then_inc(pv_done, 1)

            def prep(n, par, j, before):
                before()
                if j == 0:
                    pe.wait_ge(w_scaled, n + 1)
                    pe.wait_ge(loaded, 16 * LOADS * (n + 1))
                alone(pe)
                jobs[j][1](n, par).then_inc(prep_ready, 1)

            def tail(n, half, which, before):
                before()
                if which == 0:
                    pe.wait_ge(tail_dve, 4 * n + 2 * half + 1)
                    alone(pe)
                    for cc in range(4):
                        last = nc.tensor.matmul(M[:, P * cc:P * cc + P],
                                                inverse_wide[:, G * cc:G * cc + G, :].rearrange("p g x -> p (g x)"),
                                                ident_sb[:], start=True, stop=True)
                else:
                    if which == 1:
                        pe.wait_ge(tail_dve, 4 * n + 2 * half + 2)
                        if half == 0:
                            pe.wait_ge(wo_loaded, 16 * n + 16)
                    m = which - 1
                    last = nc.tensor.matmul(M[0:HALF, :], wo_sb[:, m * HALF:(m + 1) * HALF],
                                            OSB[:], start=True, stop=True)
                last.then_inc(tail_ready, 1)

            def prologue():
                pe.wait_ge(consts_loaded, 16 * len(const))
                pe.wait_ge(prepared, 1)
                for j in range(NJ):
                    prep(0, 0, j, (lambda j=j: prep_out(pe, 0, j - 1)) if j else (lambda: None))

            def body(u, par, first, last):
                prep_out(pe, u, NJ - 1)
                if not rel:
                    pe.wait_ge(k_loaded, 16 * len(PAIRS) * (u + 1))
                    pe.wait_ge(q_loaded[0], 16 * len(PAIRS) * (u + 1))
                    alone(pe)
                scores(u, par, range(2))
                if SLOTS == 4:
                    scores(u, par, range(2, 4))
                before = (lambda: prep_out(pe, 0, NJ - 1)) if first else (lambda: tail_out(pe, u - 1, 0, 2))
                for t in range(TILES):
                    if t + SLOTS < TILES:
                        scores(u, par, [t + SLOTS])
                    turn(u, t)
                    if t % 4 == LAG:
                        if t >= 4:
                            output(u, par, t // 4 - 1)
                        elif not first:
                            output(u - 1, 1 - par, CHUNKS - 1)
                    if t in TAIL_AFTER and not first:
                        half, which = TAIL_AFTER[t]
                        tail(u - 1, half, which, before)
                        before = lambda half=half, which=which: tail_out(pe, u - 1, half, which)
                    if t in job_at and not last:
                        j = job_at[t]
                        prep(u + 1, 1 - par, j, before)
                        before = lambda j=j: prep_out(pe, u + 1, j)
                    if t in TAIL_AT:
                        half, which = TAIL_AT[t]
                        tail(u, half, which, before)
                        before = lambda half=half, which=which: tail_out(pe, u, half, which)

            def epilogue():
                n = UNITS - 1
                output(n, 1, CHUNKS - 1)
                before = lambda: tail_out(pe, n, 0, 2)
                for half, which in TAIL_AFTER.values():
                    tail(n, half, which, before)
                    before = lambda half=half, which=which: tail_out(pe, n, half, which)

            pairs(pe, prologue, body, epilogue)

        @block.vector
        def _(eng):
            def scale_k(n):
                eng.wait_ge(loaded, 16 * LOADS * (n + 1))
                for ap in scaled:
                    last = nc.vector.tensor_scalar(ap, ap, SCALE, None, ALU.mult)
                last.then_inc(w_scaled, 1)

            def prep(n, par, j):
                if not jobs[j][2]:
                    return
                eng.wait_ge(prep_ready, NJ * n + j + 1)
                done = sum(count_dve[:j])
                for f in jobs[j][2]:
                    if f == "wait":
                        eng.wait_ge(prep_dve, PD * n + done)
                        alone(eng)
                    elif not callable(f):
                        free_whole(n, f[1])
                    else:
                        f(par).then_inc(prep_dve, 1)
                        done += 1

            def invert(n, half):
                eng.wait_ge(exp_done, TILES * n + 16 * half + 16)
                nc.vector.reciprocal(inverse[:], sums[:, 16 * half:16 * half + 16]).then_inc(inverted, 1)
                eng.wait_ge(inverted, 2 * n + half + 1)
                nc.vector.tensor_copy(inverse_wide[:], inverse[:].unsqueeze(2).to_broadcast([P, TILES // 2, Q])
                                      ).then_inc(tail_dve, 1)

            def tail(n, half, which):
                if which:
                    return
                eng.wait_ge(o_out, 2 * n + half + 1)
                eng.wait_ge(tail_ready, 6 * n + 3 * half + 1)
                nc.vector.tensor_tensor(OSB[:], M[:], OSB[:], ALU.mult).then_inc(tail_dve, 1)

            def row_max(u, t):
                c, g = divmod(t, G)
                T = TILES * u + t
                eng.wait_ge(s_ready, T + 1)
                if rel:
                    nc.vector.tensor_reduce(nmax[:, t % 4:t % 4 + 1], S[:, t % SLOTS, :], AX.X, ALU.max,
                                            negate=True).then_inc(max_done, 1)
                    return
                need(eng, turned, TURNS * (T - PROBS + 1))
                if window:
                    add = mask_sb[:, 0 if c == 0 else 2 if c == CHUNKS - 1 else 1, :]
                else:
                    add = mask_sb[:, g, c, :]
                    if g == 0 and c % (CHUNKS // 2) == 0:
                        eng.wait_ge(mask_loaded[c // (CHUNKS // 2)], MASKS * (u + 1))
                alone(eng)
                nc.vector.tensor_tensor_reduce(out=PROB[:, t % PROBS, :], in0=S[:, t % SLOTS, :], in1=add, scale=-1.0,
                                               scalar=BIG, op0=ALU.add, op1=ALU.min,
                                               accum_out=nmax[:, t % 4:t % 4 + 1]).then_inc(max_done, 1)

            def evacuate(u, t):
                if window and t % 2:
                    return
                c, g = divmod(t, G)
                eng.wait_ge(turned, TURNS * (TILES * u + t) + 1)
                if g == 0:
                    need(eng, pv_done, CHUNKS * u + c - PTSLOTS + 1)
                nc.vector.tensor_copy(PTS[:, c % PTSLOTS, g, 0:BANK], PT[:, 0, :]).then_inc(evac_dve, 1)

            def prologue():
                nc.vector.memset(O[:], 0.0).then_inc(prepared, 1)
                if not rel:
                    eng.wait_ge(consts_loaded, 16 * len(const))
                scale_k(0)
                for j in range(NJ):
                    prep(0, 0, j)

            def body(u, par, first, last):
                for t in range(SLOTS):
                    if t < 2 or window:
                        row_max(u, t)
                for t in range(TILES):
                    if not rotary and t + SLOTS < TILES:
                        row_max(u, t + SLOTS)
                    if t == 1 and not first:
                        invert(u - 1, 1)
                    if t == 5 and not last:
                        scale_k(u + 1)
                    if t - 1 in TAIL_AFTER and not first:
                        tail(u - 1, *TAIL_AFTER[t - 1])
                    if t - 1 in job_at and not last:
                        prep(u + 1, 1 - par, job_at[t - 1])
                    if t - 1 in TAIL_AT:
                        tail(u, *TAIL_AT[t - 1])
                    evacuate(u, t)
                    if t == 19:
                        invert(u, 0)
                    if rotary and t + 2 < TILES:
                        row_max(u, t + 2)

            def epilogue():
                n = UNITS - 1
                invert(n, 1)
                tail(n, 1, 0)

            pairs(eng, prologue, body, epilogue)

        @block.scalar
        def _(act):
            def prep(n, par, j):
                if not jobs[j][3]:
                    return
                act.wait_ge(prep_ready, NJ * n + j + 1)
                for f in jobs[j][3]:
                    f(par).then_inc(prep_act, 1)

            def tail(n, half, which):
                if not which:
                    return
                k = 2 * half + which - 1
                act.wait_ge(tail_ready, 6 * n + 3 * half + which + 1)
                need(act, y_stored[k % YS], 16 * (4 // YS * n + k // YS))
                nc.scalar.copy(Y[:, k % YS, :], M[0:HALF, :]).then_inc(tail_act, 1)

            def exponential(u, t):
                T = TILES * u + t
                act.wait_ge(max_done, T + 1)
                if rel:
                    need(act, turned, TURNS * (T - PROBS + 1))
                src = S[:, t % SLOTS, :] if rel else PROB[:, t % PROBS, :]
                nc.scalar.activation(PROB[:, t % PROBS, :], src, ACT.Exp, bias=nmax[:, t % 4:t % 4 + 1],
                                     scale=1.0 if rel else -1.0, accum_out=sums[:, t:t + 1]).then_inc(exp_done, 1)

            def evacuate(u, t):
                if window and t % 2 == 0:
                    return
                c, g = divmod(t, G)
                act.wait_ge(turned, TURNS * (TILES * u + t + 1))
                if g == (1 if window else 0):
                    need(act, pv_done, CHUNKS * u + c - PTSLOTS + 1)
                k0 = 0 if window else BANK
                nc.scalar.copy(PTS[:, c % PTSLOTS, g, k0:k0 + BANK], PT[:, 1, :]).then_inc(evac_act, 1)

            def outputs(u, half):
                act.wait_ge(pv_done, CHUNKS * u + 4 * half + 4)
                nc.scalar.copy(OSB[:], O[:]).then_inc(o_out, 1)

            def prologue():
                for j in range(NJ):
                    prep(0, 0, j)

            def body(u, par, first, last):
                exponential(u, 0)
                for t in range(TILES):
                    if t + 1 < TILES:
                        exponential(u, t + 1)
                    if t == 2 and not first:
                        outputs(u - 1, 1)
                    if t - 1 in TAIL_AFTER and not first:
                        tail(u - 1, *TAIL_AFTER[t - 1])
                    if t - 1 in job_at and not last:
                        prep(u + 1, 1 - par, job_at[t - 1])
                    if t - 1 in TAIL_AT:
                        tail(u, *TAIL_AT[t - 1])
                    if t == 18:
                        outputs(u, 0)
                    evacuate(u, t)

            def epilogue():
                n = UNITS - 1
                outputs(n, 1)
                tail(n, 1, 1)
                tail(n, 1, 2)

            pairs(act, prologue, body, epilogue)


def program(nc, a, out):
    def scratch(n):
        return nc.dram_tensor(n, (IMAGES, HALF, 2, TOKENS), F32).ap()

    xn = scratch("xn_scratch")
    streams = [scratch(f"stream{i}") for i in range(3)] + [out]
    x = a["x"]
    sems = ExitStack()
    for i, kind in enumerate(("rel", "window", "rel", "rotary")):
        pre = f"L{i}_"
        w = {n[3:]: ap for n, ap in a.items() if n.startswith(pre)}
        lepe = {"wv": w["wv_all"], "bv": w["bv_all"], "lw": w["lw"], "lb": w["lb"], "wo": w["wo_all"]} if i == 3 else None
        normalise_block(nc, sems, f"n{i}", x, xn, streams[i], w["bo"], a["gavg"], lepe)
        attend_block(nc, sems, f"a{i}", kind, xn, streams[i], w, a["ident"])
        x = streams[i]
    sems.close()


def _halves(w):
    return w.reshape(2, HALF, -1).transpose(1, 0, 2)


def _by_group(w):
    return _halves(w).reshape(HALF, 2, GROUPS, G * DIM).transpose(2, 0, 1, 3)


def _spread_heads(w):
    z = np.zeros(w.shape[:-1] + (G, Q), w.dtype)
    z[..., 0:DIM] = w.reshape(w.shape[:-1] + (G, DIM))
    return z.reshape(w.shape[:-1] + (P,))


def _turn_pairs(w):
    return w.reshape(w.shape[:-1] + (-1, 2))[..., ::-1].reshape(w.shape)


def _layouts(inp):
    f = np.float32
    a = {}
    a["x"] = inp["x"].reshape(IMAGES, TOKENS, 2, HALF).transpose(0, 3, 2, 1)
    a["ident"] = np.eye(P, dtype=f)
    group = np.arange(HALF) // 6
    a["gavg"] = ((group[:, None] == group[None, :]) / 6.0).astype(f)

    qkv = {0: inp["L0_conv_w_qkv"], 1: inp["L1_conv_qkv_w"].T, 2: inp["L2_conv_qkv_w"].T,
           3: [inp[f"L3_conv_w{n}"].T for n in "qkv"]}
    bias = {0: inp["L0_conv_b_qkv"], 1: inp["L1_conv_qkv_b"], 2: inp["L2_conv_qkv_b"],
            3: [inp[f"L3_conv_b{n}"] for n in "qkv"]}
    wo = {0: inp["L0_conv_w_proj"], 1: inp["L1_conv_out_w"].T, 2: inp["L2_conv_proj_w"].T, 3: inp["L3_conv_wo"].T}
    bo = {0: inp["L0_conv_b_proj"], 1: inp["L1_conv_out_b"], 2: inp["L2_conv_proj_b"], 3: inp["L3_conv_bo"]}
    for i in range(4):
        if i == 3:
            (wq, wk, wv), (bq, bk, bv) = qkv[3], bias[3]
        else:
            wq, wk, wv = (qkv[i][:, n * CHANNELS:(n + 1) * CHANNELS] for n in range(3))
            bq, bk, bv = (bias[i][n * CHANNELS:(n + 1) * CHANNELS] for n in range(3))
        def by(b):
            return b.reshape(GROUPS, G * DIM)
        p = f"L{i}_"
        a[p + "wv"], a[p + "bv"] = _by_group(wv), by(bv)[:, :, None]
        a[p + "wo"] = _spread_heads(wo[i].T.reshape(CHANNELS, GROUPS, G * DIM).transpose(1, 0, 2)).transpose(0, 2, 1)
        a[p + "bo"] = bo[i].reshape(2, HALF).T
        if i in (0, 2):
            a[p + "wqk"] = np.concatenate([_by_group(wq), _by_group(wk)], axis=-1)
            a[p + "bqk"] = np.concatenate([by(bq), by(bk)], axis=-1)[:, :, None]
            rh = inp[f"L{i}_conv_rel_pos_h"][::-1].T
            rw = inp[f"L{i}_conv_rel_pos_w"][::-1].T
            tab = np.zeros((DIM, 2, SIDE, Q), f)
            for v in range(2):
                for row in range(SIDE):
                    tab[:, v, row, 0:DIM] = np.eye(DIM, dtype=f)
                    k = SIDE - 1 - row + DIM * v
                    tab[:, v, row, DIM:] = rh[:, k:k + DIM]
            a[p + "tab_h"], a[p + "tab_w"] = tab, rw
            key = np.arange(BANK)
            one = np.zeros((3 * Q, 2, BANK), f)
            one[DIM + key // SIDE, 0, key] = 1
            one[2 * Q + DIM + key // SIDE, 1, key] = 1
            one[Q + key % SIDE, :, key] = 1
            a[p + "onehot"] = one
        else:
            for n, turned in (("qk", lambda t: t), ("qkr", _turn_pairs)):
                if n == "qk" or i == 3:
                    a[p + "w" + n] = np.concatenate([_by_group(turned(wq)), _by_group(turned(wk))], axis=-1)
                    a[p + "b" + n] = np.concatenate([by(turned(bq)), by(turned(bk))], axis=-1)[:, :, None]
        if i == 1:
            regs = np.zeros((CHANNELS, P), f)
            regs[:, 0:REGS] = inp["L1_conv_registers"].T
            a[p + "regs"] = _halves(regs)
            mask = np.full((P, 3, KEYS_W), -1e30, f)
            for n, c, k0 in ((0, 0, 0), (1, 1, 0), (2, CHUNKS - 1, CHUNKS - 3)):
                q, k = P * c + np.arange(P), P * k0 + np.arange(3 * P)
                ok = np.ones((P, 3 * P), bool)
                for qi, ki in ((q // SIDE, k // SIDE), (q % SIDE, k % SIDE)):
                    start = np.clip(qi - WINDOW // 2, 0, SIDE - WINDOW)[:, None]
                    ok &= (ki[None, :] >= start) & (ki[None, :] < start + WINDOW)
                mask[:, n, 0:3 * P][ok] = 0
                mask[:, n, 3 * P:3 * P + REGS] = 0
            a[p + "mask"] = mask
        if i == 3:
            a[p + "wv_all"], a[p + "bv_all"] = _halves(wv), bv.reshape(2, HALF).T
            a[p + "wo_all"] = _halves(wo[3])
            a[p + "lw"] = inp["L3_conv_lepe_w"].reshape(TAPS * TAPS, 2, HALF).transpose(2, 1, 0)
            a[p + "lb"] = inp["L3_conv_lepe_b"].reshape(2, HALF).T
            for n in ("sin", "cos"):
                a[p + n] = np.tile(inp[f"L3_conv_{n}"].reshape(TOKENS, DIM).T, (P // DIM, 1))
            a[p + "sign"] = np.where(np.arange(P) % 2, 1.0, -1.0).astype(f)[:, None]
            a[p + "mask"] = inp["L3_conv_mask"].reshape(GROUPS, G, CHUNKS, P, TOKENS).transpose(0, 2, 3, 1, 4)
    return {n: np.ascontiguousarray(v) for n, v in a.items()}


def kernel(**inputs):
    import concourse.bacc as _bacc
    from concourse.bass_utils import run_bass_kernel_spmd as _run

    arrays = _layouts({n: np.asarray(v) for n, v in inputs.items()})
    nc = _bacc.Bacc("TRN2", target_bir_lowering=False, num_devices=1)
    aps = {n: nc.dram_tensor(n, v.shape, mybir.dt.from_np(v.dtype), kind="ExternalInput").ap() for n, v in arrays.items()}
    out = nc.dram_tensor("out", (IMAGES, HALF, 2, TOKENS), F32, kind="ExternalOutput").ap()
    program(nc, aps, out)
    r = _run(nc, [arrays], core_ids=[0])
    y = r.results[0]["out"]
    return y.transpose(0, 3, 2, 1).reshape(IMAGES, SIDE, SIDE, CHANNELS)
```

```python
from contextlib import ExitStack

import numpy as np

import concourse.bass as bass
from concourse import mybir

ALU = mybir.AluOpType
ACT = mybir.ActivationFunctionType
AX = mybir.AxisListType
F32, BF16 = mybir.dt.float32, mybir.dt.bfloat16

P = 128
IMAGES, SIDE, CHANNELS, HEADS = 8, 32, 192, 12
TOKENS = SIDE * SIDE
DIM = CHANNELS // HEADS
GROUPS = 3
G = HEADS // GROUPS
HALF = CHANNELS // 2
CHUNKS = TOKENS // P
TILES = CHUNKS * G
Q = 32
BANK = 512
SCALE = float(DIM) ** -0.5
WINDOW, REGS = 7, 16
KEYS_W = 4 * P
BIG = 3.0e38
TAPS = 5
PAD = SIDE + TAPS - 1
GN_EPS = 1e-5
PAIRS = ((0, 0), (0, 1), (1, 0), (0, 2), (2, 0), (1, 1))
PARTS = 3


def alone(eng):
    eng.nop(nofuse=True)


def need(eng, sem, value, solo=False):
    if isinstance(value, int) and value <= 0:
        return
    eng.wait_ge(sem, value)
    if solo:
        alone(eng)


def images(eng, body):
    body(0, 0, False)
    body(1, 1, False)
    with eng.Fori(1, IMAGES // 2 - 1) as p:
        body(2 * p, 0, False)
        body(2 * p + 1, 1, False)
    body(IMAGES - 2, 0, False)
    body(IMAGES - 1, 1, True)


def normalise_block(nc, sems, name, x_in, xn_out, stream_out, bias, gavg, lepe=None):
    with ExitStack() as ctx:
        def sb(n, shape):
            return ctx.enter_context(nc.sbuf_tensor(f"{name}_{n}", shape, F32))

        def sem(n):
            return sems.enter_context(nc.semaphore(f"{name}_{n}"))

        X2 = sb("x", [HALF, 2, 2, TOKENS])
        XN2 = sb("xn", [HALF, 2, 2, TOKENS])
        ST2 = sb("stream", [HALF, 2, 2, TOKENS])
        bias_sb = sb("bias", [HALF, 2])
        gavg_sb = sb("gavg", [HALF, HALF])
        stats = sb("stats", [HALF, 2, 2, 6])
        mv = sb("mv", [HALF, 2, 2])
        sq = sb("sq", [HALF, 2])
        me = sb("me", [HALF, 2, 2])
        gm = sb("gm", [HALF, 2, 2])
        gsq = sb("gsq", [HALF, 2])
        var = sb("var", [HALF, 2])
        power = sb("power", [HALF, 2])
        rstd = sb("rstd", [HALF, 2])
        ps_g = ctx.enter_context(nc.psum_tensor(f"{name}_psg", [P, BANK], F32))
        loaded_c = sem("loaded_c")
        loaded_x = sem("loaded_x")
        stored_xn = sem("stored_xn")
        stored_st = sem("stored_st")
        power_set = sem("power_set")
        dve = sem("dve")
        averaged = sem("averaged")
        powered = sem("powered")
        xn_ready = sem("xn_ready")
        st_ready = sem("st_ready")
        if lepe:
            VP = sb("vpad", [HALF, 2, PAD, PAD])
            CV = sb("conv", [HALF, 2, TOKENS])
            wv_sb = sb("wv", [HALF, 2, CHANNELS])
            bv_sb = sb("bv", [HALF, 2])
            lw_sb = sb("lw", [HALF, 2, TAPS * TAPS])
            lb_sb = sb("lb", [HALF, 2])
            wo_sb = sb("wo", [HALF, 2, CHANNELS])
            ps_v = ctx.enter_context(nc.psum_tensor(f"{name}_psv", [P, 4, BANK], F32))
            v_ready = sem("v_ready")
            v_padded = sem("v_padded")
            pad_set = sem("pad_set")
            taps = sem("taps")
            o_ready = sem("o_ready")
            st_added = sem("st_added")
        consts = 2 + (5 if lepe else 0)
        DVE_STEPS = 11
        NT = 2 * TAPS * TAPS
        block = ctx.enter_context(nc.Block())

        @block.sync
        def _(sp):
            sp.dma_start(bias_sb[:], bias).then_inc(loaded_c, 16)
            sp.dma_start(gavg_sb[:], gavg).then_inc(loaded_c, 16)
            if lepe:
                for dst, src in ((wv_sb, "wv"), (bv_sb, "bv"), (lw_sb, "lw"), (lb_sb, "lb"), (wo_sb, "wo")):
                    sp.dma_start(dst[:], lepe[src]).then_inc(loaded_c, 16)
            sp.dma_start(X2[:, 0], x_in[0]).then_inc(loaded_x, 16)

            def image(b, slot, last):
                sp.wait_ge(loaded_x, 16 * b + 16)
                alone(sp)
                if not last:
                    need(sp, xn_ready, 2 * b)
                    need(sp, st_ready, b)
                    alone(sp)
                    sp.dma_start(X2[:, 1 - slot], x_in[b + 1]).then_inc(loaded_x, 16)
                sp.wait_ge(xn_ready, 2 * b + 2)
                need(sp, stored_xn, 16 * b)
                alone(sp)
                sp.dma_start(xn_out[b], XN2[:, slot]).then_inc(stored_xn, 16)
                sp.wait_ge(st_ready, b + 1)
                if lepe:
                    sp.wait_ge(st_added, 2 * b + 2)
                alone(sp)
                need(sp, stored_st, 16 * b)
                alone(sp)
                sp.dma_start(stream_out[b], ST2[:, slot]).then_inc(stored_st, 16)

            images(sp, image)
            sp.wait_ge(stored_xn, 16 * IMAGES)
            sp.wait_ge(stored_st, 16 * IMAGES)

        @block.vector
        def _(eng):
            if lepe:
                nc.vector.memset(VP[:], 0.0).then_inc(pad_set, 1)

            def image(b, slot, last):
                X, XN, ST = X2[:, slot], XN2[:, slot], ST2[:, slot]
                base = b * DVE_STEPS
                eng.wait_ge(loaded_x, 16 * b + 16)
                for m in range(2):
                    for h in range(2):
                        nc.vector.bn_stats(stats[:, m, h, :], X[:, m, h * BANK:(h + 1) * BANK]).then_inc(dve, 1)
                eng.wait_ge(dve, base + 4)
                alone(eng)
                for m in range(2):
                    nc.vector.bn_aggr(mv[:, m, :], stats[:, m, :, :].rearrange("p a b -> p (a b)")).then_inc(dve, 1)
                eng.wait_ge(dve, base + 6)
                nc.vector.tensor_tensor(sq[:], mv[:, :, 0], mv[:, :, 0], ALU.mult).then_inc(dve, 1)
                nc.vector.tensor_copy(me[:, :, 0], mv[:, :, 0]).then_inc(dve, 1)
                eng.wait_ge(dve, base + 8)
                nc.vector.tensor_tensor(me[:, :, 1], sq[:], mv[:, :, 1], ALU.add).then_inc(dve, 1)
                eng.wait_ge(averaged, b + 1)
                nc.vector.tensor_copy(gm[:], ps_g[0:HALF, 0:4].rearrange("p (a b) -> p a b", a=2)).then_inc(dve, 1)
                eng.wait_ge(dve, base + 10)
                nc.vector.tensor_tensor(gsq[:], gm[:, :, 0], gm[:, :, 0], ALU.mult).then_inc(dve, 1)
                eng.wait_ge(dve, base + 11)
                nc.vector.scalar_tensor_tensor(out=var[:], in0=gm[:, :, 1], scalar=GN_EPS, in1=gsq[:],
                                               op0=ALU.add, op1=ALU.subtract).then_inc(power_set, 1)
                eng.wait_ge(powered, b + 2)
                need(eng, stored_xn, 16 * (b - 1))
                alone(eng)
                for m in range(2):
                    nc.vector.tensor_scalar(XN[:, m, :], X[:, m, :], gm[:, m, 0:1], rstd[:, m:m + 1],
                                            ALU.subtract, ALU.mult).then_inc(xn_ready, 1)
                if lepe:
                    eng.wait_ge(v_padded, 2 * b + 2)
                    for k in range(TAPS * TAPS):
                        dy, dx = divmod(k, TAPS)
                        for m in range(2):
                            n = NT * b + 2 * k + m
                            src = VP[:, m, dy:dy + SIDE, dx:dx + SIDE]
                            dst = CV[:, m, :].rearrange("p (a b) -> p a b", a=SIDE)
                            if k == 0:
                                ins = nc.vector.tensor_scalar(dst, src, lw_sb[:, m, 0:1], lb_sb[:, m:m + 1],
                                                              ALU.mult, ALU.add)
                            else:
                                need(eng, taps, n - 1)
                                ins = nc.vector.scalar_tensor_tensor(out=dst, in0=src, scalar=lw_sb[:, m, k:k + 1],
                                                                     in1=dst, op0=ALU.mult, op1=ALU.add)
                            ins.then_inc(taps, 1)
                    eng.wait_ge(o_ready, b + 1)
                    eng.wait_ge(st_ready, b + 1)
                    for m in range(2):
                        nc.vector.tensor_tensor(ST[:, m, :], ps_v[0:HALF, 2 * m:2 * m + 2, :].rearrange("p a b -> p (a b)"),
                                                ST[:, m, :], ALU.add).then_inc(st_added, 1)

            images(eng, image)

        @block.tensor
        def _(pe):
            pe.wait_ge(loaded_c, 16 * consts)

            def image(b, slot, last):
                XN = XN2[:, slot]
                pe.wait_ge(dve, b * DVE_STEPS + 9)
                nc.tensor.matmul(ps_g[0:HALF, 0:4], gavg_sb[:], me[:].rearrange("p a b -> p (a b)"),
                                 start=True, stop=True).then_inc(averaged, 1)
                if lepe:
                    pe.wait_ge(xn_ready, 2 * b + 2)
                    for m in range(2):
                        for t in range(2):
                            for k in range(2):
                                last = nc.tensor.matmul(ps_v[0:HALF, 2 * m + t, :], wv_sb[:, k, m * HALF:(m + 1) * HALF],
                                                        XN[:, k, t * BANK:(t + 1) * BANK], start=k == 0, stop=k == 1)
                    last.then_inc(v_ready, 1)
                    pe.wait_ge(taps, NT * b + NT)
                    pe.wait_ge(v_padded, 2 * b + 2)
                    for m in range(2):
                        for t in range(2):
                            for k in range(2):
                                last = nc.tensor.matmul(ps_v[0:HALF, 2 * m + t, :], wo_sb[:, k, m * HALF:(m + 1) * HALF],
                                                        CV[:, k, t * BANK:(t + 1) * BANK], start=k == 0, stop=k == 1)
                    last.then_inc(o_ready, 1)
                    pe.wait_ge(st_added, 2 * b + 2)
                    alone(pe)

            images(pe, image)

        @block.scalar
        def _(act):
            act.wait_ge(loaded_c, 16 * consts)
            if lepe:
                act.wait_ge(pad_set, 1)

            def image(b, slot, last):
                X, ST = X2[:, slot], ST2[:, slot]
                act.wait_ge(loaded_x, 16 * b + 16)
                alone(act)
                need(act, stored_st, 16 * (b - 1), solo=True)
                nc.scalar.activation(ST[:, 0, :], X[:, 0, :], ACT.Identity, bias=bias_sb[:, 0:1])
                nc.scalar.activation(ST[:, 1, :], X[:, 1, :], ACT.Identity, bias=bias_sb[:, 1:2]).then_inc(st_ready, 1)
                if lepe:
                    act.wait_ge(v_ready, b + 1)
                    for m in range(2):
                        nc.scalar.activation(VP[:, m, 2:2 + SIDE, 2:2 + SIDE],
                                             ps_v[0:HALF, 2 * m:2 * m + 2, :].rearrange("p a (y x) -> p (a y) x", x=SIDE),
                                             ACT.Identity, bias=bv_sb[:, m:m + 1]).then_inc(v_padded, 1)

            images(act, image)

        @block.gpsimd
        def _(pool):
            nc.gpsimd.memset(power[:], -0.5).then_inc(powered, 1)
            pool.wait_ge(powered, 1)
            with pool.Fori(0, IMAGES) as b:
                pool.wait_ge(power_set, b + 1)
                nc.gpsimd.tensor_tensor(rstd[:], var[:], power[:], ALU.pow).then_inc(powered, 1)


def attend_block(nc, sems, name, kind, xn, stream, w, ident):
    rel, window, rotary = kind == "rel", kind == "window", kind == "rotary"
    KTOK = TOKENS + (P if window else 0)
    VC = KTOK // P
    KEYS = KEYS_W if window else TOKENS
    SLOTS = 4 if window else 2
    PROBS = 2 if rotary else 4
    PTSLOTS = 5 if rotary else 8
    UNITS = GROUPS * IMAGES
    YS = 1 if rotary else 2
    LAG = 0 if rotary else 1
    WIDTHS = [BANK, BANK] + ([P] if window else [])
    PIECES = len(WIDTHS)
    STARTS = [BANK * i for i in range(PIECES)]
    with ExitStack() as ctx:
        def sb(n, shape, dt=F32):
            return ctx.enter_context(nc.sbuf_tensor(f"{name}_{n}", shape, dt))

        def sem(n):
            return sems.enter_context(nc.semaphore(f"{name}_{n}"))

        S = ctx.enter_context(nc.psum_tensor(f"{name}_S", [P, SLOTS, KEYS], F32))
        PT = ctx.enter_context(nc.psum_tensor(f"{name}_PT", [P, 2, BANK], F32))
        O = ctx.enter_context(nc.psum_tensor(f"{name}_O", [P, BANK], F32))
        M = ctx.enter_context(nc.psum_tensor(f"{name}_M", [P, BANK], F32))

        ident_sb = sb("ident", [P, P])
        wo_sb = sb("wo", [P, CHANNELS])
        wv_sb = sb("wv", [HALF, 2, G * DIM])
        bv_sb = sb("bv", [G * DIM, 1])
        XTOK = BANK if rotary else KTOK
        X = sb("X", [HALF, 2, XTOK])
        PTS = sb("PTS", [P, PTSLOTS, KEYS])
        OSB = sb("OSB", [P, BANK])
        Y = sb("Y", [HALF, YS, BANK])
        VT = OSB[0:G * DIM, :] if rotary else sb("VT", [G * DIM, BANK])[:]
        V = sb("V", [P, 2, VC, G, DIM])
        PROB = sb("PROB", [P, PROBS, KEYS])
        nmax = sb("nmax", [P, 4])
        sums = sb("sums", [P, TILES])
        inverse = sb("inverse", [P, TILES // 2])
        KK = sb("KK", [P if rel else DIM * len(PAIRS), 2, G, KTOK], BF16)
        if rel:
            QQ = sb("QQ", [P, 2, 2, G, TOKENS], BF16)
            QREL = sb("QREL", [P, 2, G, TOKENS], BF16)
            KREL = sb("KREL", [P, TOKENS], BF16)
            QC = sb("QC", [DIM, G, TOKENS])
            RHW = sb("RHW", [2 * Q, G, TOKENS])
            RP = sb("RP", [2 * Q, PARTS, G, TOKENS], BF16)
            tab_h = sb("tab_h", [DIM, 2 * SIDE - 1])
            tab_w = sb("tab_w", [DIM, 2 * SIDE - 1])
        else:
            QQ = sb("QQ", [DIM * len(PAIRS), G, TOKENS], BF16)
        whole = sb("whole", [P, BANK])
        inverse_wide = (whole if rotary else sb("inverse_wide", [P, BANK]))[:].rearrange("p (t x) -> p t x", x=Q)
        split_parts = sb("split_parts", [P, PARTS, BANK], BF16)
        parts = nc.dram_tensor(f"{name}_parts", (2, PARTS, P, KTOK), BF16).ap()
        weights = {}
        for n in ["qk"] + (["qkr"] if rotary else []):
            weights["w" + n] = sb("w" + n, [HALF, 2, P])
            weights["b" + n] = sb("b" + n, [P, 1])
        scaled = [(t[:, :, 64:] if n[0] == "w" else t[64:, :]) for n, t in weights.items()]
        if window:
            mask_sb = sb("mask", [P, 3, KEYS_W])
        if rotary:
            mask_sb = sb("mask", [P, G, CHUNKS, TOKENS])
            cos_sb = sb("cos", [P, BANK])
            sin_sb = sb("sin", [P, BANK])
            sign_sb = sb("sign", [P, 1])
        weights |= {"wv": wv_sb, "bv": bv_sb}
        NW = len(weights)
        const = {"ident": (ident_sb[:], ident)}
        if rel:
            const |= {"tab_h": (tab_h[:], w["tab_h"]), "tab_w": (tab_w[:], w["tab_w"])}
            const |= {"ones": (PROB[:, 0, :], w["ones"]), "ones_rel": (PROB[:, 1, :], w["ones_rel"])}
        if window:
            const |= {"mask": (mask_sb[:], w["mask"]), "regs": (X[:, :, TOKENS:], w["regs"])}
        if rotary:
            const |= {"sign": (sign_sb[:], w["sign"])}

        consts_loaded = sem("consts_loaded")
        loaded = sem("loaded")
        w_scaled = sem("w_scaled")
        PREPARED = 1 + (1 + 2 * G if rel else 0)
        loaded_more = sem("loaded_more") if rotary else None
        moved = sem("moved") if rel else None
        rel_moved = sem("rel_moved") if rel else None
        REL_MOVES = 8
        split = sem("split")
        parts_stored = sem("parts_stored")
        k_loaded = sem("k_loaded")
        QK_LOADS = len(PAIRS) * (3 if rel else 1)
        if not rel:
            q_loaded = [sem(f"q_loaded{h}") for h in range(2)]
        SPLIT_STEPS, REL_STEPS = 4, 3 * G if rel else 0
        UNIT_STEPS = SPLIT_STEPS * PIECES + REL_STEPS
        prep_ready = sem("prep_ready")
        prep_dve, prep_act = sem("prep_dve"), sem("prep_act")
        tail_ready = sem("tail_ready")
        tail_dve, tail_act = sem("tail_dve"), sem("tail_act")
        s_ready = sem("s_ready")
        max_done = sem("max_done")
        exp_done = sem("exp_done")
        turned = sem("turned")
        evac_dve, evac_act = sem("evac_dve"), sem("evac_act")
        pv_done = sem("pv_done")
        o_out = sem("o_out")
        wo_loaded = sem("wo_loaded")
        y_stored = [sem(f"y_stored{s}") for s in range(YS)]
        inverted = sem("inverted")
        MASKS = 16 * CHUNKS // 2
        mask_loaded = [sem(f"mask_loaded{h}") for h in range(2)] if rotary else None
        LOADS = NW + (3 if rotary else 1)
        TURNS = 1 if window else 2
        EVACS = TILES // 2 if window else TILES
        read_done = exp_done if rel else max_done

        def pts_slot(par, t):
            return (t + (2 * par if rotary else 0)) % PTSLOTS

        def pts_free(eng, u, par, t):
            c, g = divmod(t, G)
            if not rotary:
                chunks = CHUNKS * u + c - 1
            elif t == 0 and par == 0:
                chunks = CHUNKS * u
            else:
                chunks = CHUNKS * u + (c - 1 if g == 0 else c)
            need(eng, pv_done, chunks)

        jobs = []

        def job(step, pe, dve=(), act=()):
            jobs.append((step, pe, list(dve), list(act)))

        def project(w_sb, rows, half):
            def run(n, par):
                cols = slice(STARTS[half], STARTS[half] + WIDTHS[half])
                if rotary:
                    cols = slice(0, BANK)
                    if half == 1:
                        nc.tensor.wait_ge(loaded_more, 16 * 3 * (n + 1))
                        alone(nc.tensor)
                for k in range(2):
                    last = nc.tensor.matmul(M[0:rows, 0:cols.stop - cols.start], w_sb[:, k, :], X[:, k, cols],
                                            start=k == 0, stop=k == 1)
                return last
            return run

        def v_out(half):
            width = BANK if half < 2 else P
            return lambda par: nc.scalar.activation(VT[:, 0:width], M[0:G * DIM, 0:width], ACT.Identity, bias=bv_sb[:, 0:1])

        def turn_v(half):
            blocks = 4 if half < 2 else 1

            def run(n, par):
                for j in range(blocks):
                    last = nc.tensor.transpose(M[:, 64 * j:64 * j + 64], VT[:, P * j:P * j + P],
                                               ident_sb[0:G * DIM, 0:G * DIM])
                return last

            def place(par):
                return nc.scalar.copy(V[:, par, 4 * half:4 * half + blocks, :, :],
                                      M[:, 0:64 * blocks].rearrange("p (j h d) -> p j h d", h=G, d=DIM))
            return run, place

        def add_v_jobs(step, halves):
            for i, half in enumerate(halves):
                job(step + 2 * i, project(wv_sb, G * DIM, half), act=[v_out(half)])
                run, place = turn_v(half)
                job(step + 2 * i + 1, run, act=[place])

        def free_whole(n, piece):
            before = UNIT_STEPS * n + SPLIT_STEPS * piece - (REL_STEPS if piece == 0 else 0)
            need(nc.vector, split, before, solo=True)
            if rel:
                need(nc.vector, moved, 16 * G * (PIECES * n + piece), solo=True)

        if rel:
            whole_made = []
            for piece, step in enumerate((1, 4)):
                whole_made.append(len(jobs))
                job(step, project(weights["wqk"], P, piece), dve=[
                    ("free", piece),
                    lambda par: nc.vector.tensor_scalar(whole[:], M[:], weights["bqk"][:, 0:1], None, ALU.add)])

            def relative(r):
                def run(n, par):
                    if r == 0:
                        nc.tensor.wait_ge(moved, 16 * G * PIECES * (n + 1))
                    alone(nc.tensor)
                    for il in range(4):
                        i, out = 4 * r + il, M[:, il * P:il * P + P]
                        by_row, by_col = QC[:, :, SIDE * i:SIDE * i + SIDE], QC[:, :, i:TOKENS:SIDE]
                        lines = slice(SIDE - 1 - i, 2 * SIDE - 1 - i)
                        nc.tensor.matmul(out[0:Q, :], tab_h[:, lines], by_row, start=True, stop=True)
                        last = nc.tensor.matmul(out[Q:2 * Q, :], tab_w[:, lines], by_col, start=True, stop=True)
                    return last

                def put(copy, quadrant):
                    def run(par):
                        rows = slice(Q * quadrant, Q * quadrant + Q)
                        src = M[rows].rearrange("p (i h x) -> p i h x", h=G, x=SIDE)
                        order = "p h (x i) -> p i h x" if quadrant == 1 else "p h (i x) -> p i h x"
                        to = RHW[rows].rearrange(order, **({"i": SIDE} if quadrant == 1 else {"x": SIDE}))
                        return copy(to[:, 4 * r:4 * r + 4, :, :], src)
                    return run
                job(7 + r, run, dve=[put(nc.vector.tensor_copy, 0)], act=[put(nc.scalar.copy, 1)])
            for r in range(8):
                relative(r)
            add_v_jobs(15, range(2))
            for g in range(G):
                jobs[-G + g][3].append(lambda par, g=g: nc.scalar.copy(RP[:, 0, g, :], RHW[:, g, :]))
        if window:
            whole_made = []
            for piece, step in enumerate((7, 11, 14)):
                width = WIDTHS[piece]
                whole_made.append(len(jobs))
                job(step, project(weights["wqk"], P, piece), dve=[
                    ("free", piece),
                    lambda par, width=width: nc.vector.tensor_scalar(
                        whole[:, 0:width], M[:, 0:width], weights["bqk"][:, 0:1], None, ALU.add)])
                add_v_jobs(step + 1, [piece]) if piece < 2 else add_v_jobs(15, [piece])
        if rotary:
            whole_made = []
            for piece, step in enumerate((7, 15)):
                job(step, project(weights["wqk"], P, piece), dve=[
                    ("free", piece),
                    lambda par: nc.vector.scalar_tensor_tensor(
                        out=whole[:], in0=M[:], scalar=weights["bqk"][:, 0:1], in1=cos_sb[:],
                        op0=ALU.add, op1=ALU.mult)])
                whole_made.append(len(jobs))
                job(step + 1, project(weights["wqkr"], P, piece), dve=[
                    lambda par: nc.vector.scalar_tensor_tensor(
                        out=M[:], in0=M[:], scalar=weights["bqkr"][:, 0:1], in1=sin_sb[:],
                        op0=ALU.add, op1=ALU.mult),
                    "wait",
                    lambda par: nc.vector.scalar_tensor_tensor(
                        out=whole[:], in0=M[:], scalar=sign_sb[:, 0:1], in1=whole[:],
                        op0=ALU.mult, op1=ALU.add)])
                add_v_jobs(step + 2, [piece])
        NJ = len(jobs)
        count_dve = [sum(callable(f) for f in j[2]) for j in jobs]
        count_act = [len(j[3]) for j in jobs]
        PD, PA = sum(count_dve), sum(count_act)
        job_at = {j[0]: i for i, j in enumerate(jobs)}
        assert len(job_at) == NJ

        TAIL_AT = {22: (0, 0), 24: (0, 1), 26: (0, 2)}
        TAIL_AFTER = {3: (1, 0), 4: (1, 1), 6: (1, 2)}

        def prep_out(eng, n, j):
            need(eng, prep_dve, n * PD + sum(count_dve[:j + 1]))
            need(eng, prep_act, n * PA + sum(count_act[:j + 1]), solo=True)

        def tail_out(eng, n, half, which):
            if which == 0:
                need(eng, tail_dve, 4 * n + 2 * half + 2, solo=True)
            else:
                need(eng, tail_act, 4 * n + 2 * half + which, solo=True)

        block = ctx.enter_context(nc.Block())

        @block.sync
        def _(sp):
            for dst, src in const.values():
                sp.dma_start(dst, src).then_inc(consts_loaded, 16)

            def load_x(b, half, done):
                if not rotary:
                    sp.dma_start(X[:, :, 0:TOKENS], xn[b]).then_inc(done, 16)
                    return
                cols = slice(half * BANK, (half + 1) * BANK)
                sp.dma_start(X[:], xn[b][:, :, cols]).then_inc(done, 16)
                sp.dma_start(cos_sb[:], w["cos"][:, cols]).then_inc(done, 16)
                sp.dma_start(sin_sb[:], w["sin"][:, cols]).then_inc(done, 16)

            for hg in range(GROUPS):
                def load(hg, b, par, first=False):
                    n = hg * IMAGES + b
                    for nm, dst in weights.items():
                        sp.dma_start(dst[:], w[nm][hg]).then_inc(loaded, 16)
                    load_x(b, 0, loaded)
                    for piece in range(PIECES):
                        if rotary and piece == 1:
                            sp.wait_ge(prep_ready, NJ * n + NJ // 2)
                            alone(sp)
                            load_x(b, 1, loaded_more)
                        cols = slice(STARTS[piece], STARTS[piece] + WIDTHS[piece])
                        if rel:
                            sp.wait_ge(prep_dve, PD * n + sum(count_dve[:whole_made[piece] + 1]))
                            alone(sp)
                            for g in range(G):
                                sp.dma_start(QC[:, g, cols], whole[DIM * g:DIM * g + DIM, :]).then_inc(moved, 16)
                        sp.wait_ge(split, UNIT_STEPS * n + SPLIT_STEPS * (piece + 1))
                        alone(sp)
                        sp.dma_start(parts[par, :, :, cols].rearrange("s r t -> r s t"),
                                     split_parts[:, :, 0:WIDTHS[piece]]).then_inc(parts_stored, 16)
                    sp.wait_ge(parts_stored, 16 * PIECES * (n + 1))
                    alone(sp)
                    for i, (_, part) in enumerate(PAIRS):
                        sp.dma_start(KK[DIM * i:DIM * i + DIM, par], parts[par, part, G * DIM:, :].rearrange(
                            "(g c) t -> c g t", c=DIM)).then_inc(k_loaded, 16)
                    if rel:
                        for v in range(2):
                            for i, (part, _) in enumerate(PAIRS):
                                sp.dma_start(QQ[DIM * i:DIM * i + DIM, par, v], parts[par, part, 0:G * DIM, :].rearrange(
                                    "(g c) t -> c g t", c=DIM)).then_inc(k_loaded, 16)
                        sp.wait_ge(split, UNIT_STEPS * (n + 1))
                        alone(sp)
                        for v in range(2):
                            for part in range(2):
                                to = 96 + DIM * part
                                sp.dma_start(QQ[to:to + DIM, par, v], RP[DIM * v:DIM * v + DIM, part]).then_inc(rel_moved, 16)
                        for part in range(PARTS):
                            sp.dma_start(QREL[Q * part:Q * part + Q, par], RP[Q:2 * Q, part]).then_inc(rel_moved, 16)
                        sp.dma_start(QREL[96:P, par], RP[0:Q, 2]).then_inc(rel_moved, 16)
                    for half in range(0 if rel else 2):
                        cols = slice(half * BANK, (half + 1) * BANK)
                        need(sp, s_ready, TILES * (n - 1) + TILES // 2 * (half + 1), solo=True)
                        for i, (part, _) in enumerate(PAIRS):
                            sp.dma_start(QQ[DIM * i:DIM * i + DIM, :, cols],
                                         parts[par, part, 0:G * DIM, cols].rearrange("(g c) t -> c g t", c=DIM)
                                         ).then_inc(q_loaded[half], 16)
                        if rotary and first:
                            for c in range(half * CHUNKS // 2, (half + 1) * CHUNKS // 2):
                                need(sp, max_done, TILES * (n - 1) + G * (c + 1))
                                sp.dma_start(mask_sb[:, :, c, :], w["mask"][hg, c]).then_inc(mask_loaded[half], 16)
                        elif rotary:
                            sp.wait_ge(mask_loaded[half], MASKS * n)
                            sp.sem_inc(mask_loaded[half], MASKS)
                    sp.wait_ge(prep_ready, NJ * n + NJ)
                    alone(sp)

                load(hg, 0, 0, first=True)
                load(hg, 1, 1)
                with sp.Fori(1, IMAGES // 2) as p:
                    load(hg, 2 * p, 0)
                    load(hg, 2 * p + 1, 1)

        @block.gpsimd
        def _(pool):
            def split_pieces(n):
                for piece in range(PIECES):
                    width = WIDTHS[piece]
                    rest, hi, mid, lo = (whole[:, 0:width], *(split_parts[:, i, 0:width] for i in range(PARTS)))
                    base = UNIT_STEPS * n + SPLIT_STEPS * piece
                    need(pool, parts_stored, 16 * (PIECES * n + piece), solo=True)
                    pool.wait_ge(prep_dve, PD * n + sum(count_dve[:whole_made[piece] + 1]))
                    alone(pool)
                    nc.gpsimd.tensor_copy(hi, rest).then_inc(split, 1)
                    if rel:
                        pool.wait_ge(moved, 16 * G * (PIECES * n + piece + 1))
                        alone(pool)
                    pool.wait_ge(split, base + 1)
                    alone(pool)
                    nc.gpsimd.tensor_tensor(rest, rest, hi, ALU.subtract).then_inc(split, 1)
                    pool.wait_ge(split, base + 2)
                    alone(pool)
                    nc.gpsimd.tensor_copy(mid, rest).then_inc(split, 1)
                    pool.wait_ge(split, base + 3)
                    alone(pool)
                    nc.gpsimd.tensor_tensor(lo, rest, mid, ALU.subtract).then_inc(split, 1)

            def split_relative(n):
                for g in range(G):
                    pool.wait_ge(prep_act, PA * n + PA - 2 * (G - 1 - g))
                    alone(pool)
                    base = UNIT_STEPS * n + SPLIT_STEPS * PIECES + 3 * g
                    rest, (hi, mid, lo) = RHW[:, g, :], (RP[:, i, g, :] for i in range(PARTS))
                    nc.gpsimd.tensor_tensor(mid, rest, hi, ALU.subtract).then_inc(split, 1)
                    pool.wait_ge(split, base + 1)
                    alone(pool)
                    nc.gpsimd.tensor_tensor(rest, rest, hi, ALU.subtract).then_inc(split, 1)
                    pool.wait_ge(split, base + 2)
                    alone(pool)
                    nc.gpsimd.tensor_tensor(lo, rest, mid, ALU.subtract).then_inc(split, 1)

            def store_outputs(hg, b, half):
                u = hg * IMAGES + b
                if half == 0:
                    pool.dma_start(wo_sb[:], w["wo"][hg]).then_inc(wo_loaded, 16)
                for m in range(2):
                    k = 2 * half + m
                    pool.wait_ge(tail_act, 4 * u + k + 1)
                    alone(pool)
                    pool.dma_start(stream[b][:, m, half * BANK:(half + 1) * BANK], Y[:, k % YS, :],
                                   accum_op=ALU.add).then_inc(y_stored[k % YS], 16)
                if half == 1:
                    for done in y_stored:
                        pool.wait_ge(done, 64 // YS * (u + 1))
                    alone(pool)

            def unit(hg, b):
                n = hg * IMAGES + b + 2
                store_outputs(hg, b, 0)
                if rel:
                    split_pieces(n)
                    store_outputs(hg, b, 1)
                    split_relative(n)
                else:
                    store_outputs(hg, b, 1)
                    split_pieces(n)

            for n in range(2):
                split_pieces(n)
                if rel:
                    split_relative(n)
            for hg in range(GROUPS):
                last = hg == GROUPS - 1
                with pool.Fori(0, IMAGES - 2 if last else IMAGES) as b:
                    unit(hg, b)
                if last:
                    for b in range(IMAGES - 2, IMAGES):
                        for half in range(2):
                            store_outputs(hg, b, half)

        def pairs(eng, prologue, body, epilogue):
            prologue()
            body(0, 0, True, False)
            body(1, 1, False, False)
            with eng.Fori(1, UNITS // 2 - 1) as p:
                body(2 * p, 0, False, False)
                body(2 * p + 1, 1, False, False)
            body(UNITS - 2, 0, False, False)
            body(UNITS - 1, 1, False, True)
            epilogue()

        @block.tensor
        def _(pe):
            def scores(u, par, tiles):
                todo = []
                need(pe, read_done, TILES * u + tiles[-1] - SLOTS + 1)
                for t in tiles:
                    c, g = divmod(t, G)
                    s, cols = t % SLOTS, slice(P * c, P * c + P)
                    if rel:
                        halves = [slice(h * BANK, (h + 1) * BANK) for h in range(2)]
                        todo.append([m for h, keys in enumerate(halves) for m in (
                            (S[:, s, keys], QQ[:, par, h, g, cols], KK[:, par, g, keys], True, False),
                            (S[:, s, keys], QREL[:, par, g, cols], KREL[:, keys], False, True))])
                    elif window:
                        k0 = P * min(max(c - 1, 0), CHUNKS - 3)
                        todo.append([(S[:, s, 0:3 * P], QQ[:, g, cols], KK[:, par, g, k0:k0 + 3 * P]),
                                     (S[:, s, 3 * P:], QQ[:, g, cols], KK[:, par, g, TOKENS:])])
                    else:
                        todo.append([(S[:, s, h * BANK:(h + 1) * BANK], QQ[:, g, cols],
                                      KK[:, par, g, h * BANK:(h + 1) * BANK]) for h in range(2)])
                    if not rel and t == TILES // 2:
                        pe.wait_ge(q_loaded[1], 16 * len(PAIRS) * (u + 1))
                alone(pe)
                for one in todo:
                    for out_, q_, k_, *ends in one:
                        start, stop = ends or (True, True)
                        last = nc.tensor.matmul(out_, q_, k_, start=start, stop=stop)
                    last.then_inc(s_ready, 1)

            def turn(u, t):
                T = TILES * u + t
                pe.wait_ge(exp_done, T + 1)
                for h in range(TURNS):
                    bank = t % 2 if window else h
                    if window:
                        need(pe, evac_act if t % 2 else evac_dve, EVACS * u + t // 2)
                    else:
                        need(pe, evac_act if h else evac_dve, T)
                    alone(pe)
                    for j in range(4):
                        k = BANK * h + P * j
                        last = nc.tensor.transpose(PT[:, bank, P * j:P * j + P], PROB[:, t % PROBS, k:k + P], ident_sb[:])
                    last.then_inc(turned, 1)

            def output(u, par, c):
                n = 2 * c + 2 if window else 4 * c + 4
                pe.wait_ge(evac_dve, EVACS * u + n)
                pe.wait_ge(evac_act, EVACS * u + n)
                if c % 4 == 0:
                    need(pe, o_out, 2 * u + c // 4)
                alone(pe)
                k0 = min(max(c - 1, 0), CHUNKS - 3)
                blocks = [(k0 + j, j) for j in range(3)] + [(CHUNKS, 3)] if window else [(j, j) for j in range(CHUNKS)]
                for i, (vj, j) in enumerate(blocks):
                    for g in range(G):
                        last = nc.tensor.matmul(O[Q * g:Q * g + DIM, P * (c % 4):P * (c % 4) + P], V[:, par, vj, g, :],
                                                PTS[:, pts_slot(par, G * c + g), P * j:P * j + P],
                                                start=i == 0, stop=i == len(blocks) - 1)
                last.then_inc(pv_done, 1)

            def prep(n, par, j, before):
                before()
                if j == 0:
                    pe.wait_ge(w_scaled, PREPARED + n + 1)
                    pe.wait_ge(loaded, 16 * LOADS * (n + 1))
                alone(pe)
                jobs[j][1](n, par).then_inc(prep_ready, 1)

            def tail(n, half, which, before):
                before()
                if which == 0:
                    pe.wait_ge(tail_dve, 4 * n + 2 * half + 1)
                    alone(pe)
                    for cc in range(4):
                        last = nc.tensor.matmul(M[:, P * cc:P * cc + P],
                                                inverse_wide[:, G * cc:G * cc + G, :].rearrange("p g x -> p (g x)"),
                                                ident_sb[:], start=True, stop=True)
                else:
                    if which == 1:
                        pe.wait_ge(tail_dve, 4 * n + 2 * half + 2)
                        if half == 0:
                            pe.wait_ge(wo_loaded, 16 * n + 16)
                    m = which - 1
                    last = nc.tensor.matmul(M[0:HALF, :], wo_sb[:, m * HALF:(m + 1) * HALF],
                                            OSB[:], start=True, stop=True)
                last.then_inc(tail_ready, 1)

            def prologue():
                pe.wait_ge(consts_loaded, 16 * len(const))
                pe.wait_ge(w_scaled, PREPARED)
                for j in range(NJ):
                    prep(0, 0, j, (lambda j=j: prep_out(pe, 0, j - 1)) if j else (lambda: None))

            def body(u, par, first, last):
                prep_out(pe, u, NJ - 1)
                pe.wait_ge(k_loaded, 16 * QK_LOADS * (u + 1))
                alone(pe)
                if rel:
                    pe.wait_ge(rel_moved, 16 * REL_MOVES * (u + 1))
                else:
                    pe.wait_ge(q_loaded[0], 16 * len(PAIRS) * (u + 1))
                alone(pe)
                scores(u, par, range(2))
                if SLOTS == 4:
                    scores(u, par, range(2, 4))
                before = (lambda: prep_out(pe, 0, NJ - 1)) if first else (lambda: tail_out(pe, u - 1, 0, 2))
                for t in range(TILES):
                    if window and t + SLOTS < TILES:
                        scores(u, par, [t + SLOTS])
                    turn(u, t)
                    if not window and t + SLOTS < TILES:
                        scores(u, par, [t + SLOTS])
                    if t % 4 == LAG:
                        if t >= 4:
                            output(u, par, t // 4 - 1)
                        elif not first:
                            output(u - 1, 1 - par, CHUNKS - 1)
                    if t in TAIL_AFTER and not first:
                        half, which = TAIL_AFTER[t]
                        tail(u - 1, half, which, before)
                        before = lambda half=half, which=which: tail_out(pe, u - 1, half, which)
                    if t in job_at and not last:
                        j = job_at[t]
                        prep(u + 1, 1 - par, j, before)
                        before = lambda j=j: prep_out(pe, u + 1, j)
                    if t in TAIL_AT:
                        half, which = TAIL_AT[t]
                        tail(u, half, which, before)
                        before = lambda half=half, which=which: tail_out(pe, u, half, which)

            def epilogue():
                n = UNITS - 1
                output(n, 1, CHUNKS - 1)
                before = lambda: tail_out(pe, n, 0, 2)
                for half, which in TAIL_AFTER.values():
                    tail(n, half, which, before)
                    before = lambda half=half, which=which: tail_out(pe, n, half, which)

            pairs(pe, prologue, body, epilogue)

        @block.vector
        def _(eng):
            def scale_k(n):
                eng.wait_ge(loaded, 16 * LOADS * (n + 1))
                for ap in scaled:
                    last = nc.vector.tensor_scalar(ap, ap, SCALE, None, ALU.mult)
                last.then_inc(w_scaled, 1)

            def prep(n, par, j):
                if not jobs[j][2]:
                    return
                eng.wait_ge(prep_ready, NJ * n + j + 1)
                done = sum(count_dve[:j])
                for f in jobs[j][2]:
                    if f == "wait":
                        eng.wait_ge(prep_dve, PD * n + done)
                        alone(eng)
                    elif not callable(f):
                        free_whole(n, f[1])
                    else:
                        f(par).then_inc(prep_dve, 1)
                        done += 1

            def invert(n, half, split_before=0):
                if rotary:
                    need(eng, split, split_before, solo=True)
                eng.wait_ge(exp_done, TILES * n + 16 * half + 16)
                nc.vector.reciprocal(inverse[:], sums[:, 16 * half:16 * half + 16]).then_inc(inverted, 1)
                eng.wait_ge(inverted, 2 * n + half + 1)
                nc.vector.tensor_copy(inverse_wide, inverse[:].unsqueeze(2).to_broadcast([P, TILES // 2, Q])
                                      ).then_inc(tail_dve, 1)

            def tail(n, half, which):
                if which:
                    return
                eng.wait_ge(o_out, 2 * n + half + 1)
                eng.wait_ge(tail_ready, 6 * n + 3 * half + 1)
                nc.vector.tensor_tensor(OSB[:], M[:], OSB[:], ALU.mult).then_inc(tail_dve, 1)

            def row_max(u, t):
                c, g = divmod(t, G)
                T = TILES * u + t
                eng.wait_ge(s_ready, T + 1)
                if rel:
                    nc.vector.tensor_reduce(nmax[:, t % 4:t % 4 + 1], S[:, t % SLOTS, :], AX.X, ALU.max,
                                            negate=True).then_inc(max_done, 1)
                    return
                need(eng, turned, TURNS * (T - PROBS + 1))
                if window:
                    add = mask_sb[:, 0 if c == 0 else 2 if c == CHUNKS - 1 else 1, :]
                else:
                    add = mask_sb[:, g, c, :]
                    if g == 0 and c % (CHUNKS // 2) == 0:
                        eng.wait_ge(mask_loaded[c // (CHUNKS // 2)], MASKS * (u + 1))
                alone(eng)
                nc.vector.tensor_tensor_reduce(out=PROB[:, t % PROBS, :], in0=S[:, t % SLOTS, :], in1=add, scale=-1.0,
                                               scalar=BIG, op0=ALU.add, op1=ALU.min,
                                               accum_out=nmax[:, t % 4:t % 4 + 1]).then_inc(max_done, 1)

            def evacuate(u, par, t):
                if window and t % 2:
                    return
                c, g = divmod(t, G)
                eng.wait_ge(turned, TURNS * (TILES * u + t) + 1)
                if g == 0 or (rotary and g == 1):
                    pts_free(eng, u, par, t)
                nc.vector.tensor_copy(PTS[:, pts_slot(par, t), 0:BANK], PT[:, 0, :]).then_inc(evac_dve, 1)

            def prologue():
                nc.vector.memset(O[:], 0.0).then_inc(w_scaled, 1)
                eng.wait_ge(consts_loaded, 16 * len(const))
                if rel:
                    nc.vector.tensor_copy(KREL[:], PROB[:, 1, :]).then_inc(w_scaled, 1)
                    for p in range(2):
                        for g in range(G):
                            nc.vector.tensor_copy(KK[96:P, p, g, :], PROB[96:P, 0, :]).then_inc(w_scaled, 1)
                scale_k(0)
                for j in range(NJ):
                    prep(0, 0, j)

            def body(u, par, first, last):
                for t in range(SLOTS):
                    if t < 2 or window:
                        row_max(u, t)
                for t in range(TILES):
                    if window and t + SLOTS < TILES:
                        row_max(u, t + SLOTS)
                    if t == 1 and not first:
                        invert(u - 1, 1)
                    if t == (0 if rel else 5) and not last:
                        scale_k(u + 1)
                    if t - 1 in TAIL_AFTER and not first:
                        tail(u - 1, *TAIL_AFTER[t - 1])
                    if t - 1 in job_at and not last:
                        prep(u + 1, 1 - par, job_at[t - 1])
                    if t - 1 in TAIL_AT:
                        tail(u, *TAIL_AT[t - 1])
                    evacuate(u, par, t)
                    if t == (21 if rotary else 19):
                        invert(u, 0, UNIT_STEPS * (u + (1 if last else 2)))
                    if not window and t + SLOTS < TILES:
                        row_max(u, t + SLOTS)

            def epilogue():
                n = UNITS - 1
                invert(n, 1)
                tail(n, 1, 0)

            pairs(eng, prologue, body, epilogue)

        @block.scalar
        def _(act):
            def prep(n, par, j):
                if not jobs[j][3]:
                    return
                act.wait_ge(prep_ready, NJ * n + j + 1)
                for f in jobs[j][3]:
                    f(par).then_inc(prep_act, 1)

            def tail(n, half, which):
                if not which:
                    return
                k = 2 * half + which - 1
                act.wait_ge(tail_ready, 6 * n + 3 * half + which + 1)
                need(act, y_stored[k % YS], 16 * (4 // YS * n + k // YS))
                nc.scalar.copy(Y[:, k % YS, :], M[0:HALF, :]).then_inc(tail_act, 1)

            def exponential(u, t):
                T = TILES * u + t
                act.wait_ge(max_done, T + 1)
                if rel:
                    need(act, turned, TURNS * (T - PROBS + 1))
                src = S[:, t % SLOTS, :] if rel else PROB[:, t % PROBS, :]
                nc.scalar.activation(PROB[:, t % PROBS, :], src, ACT.Exp, bias=nmax[:, t % 4:t % 4 + 1],
                                     scale=1.0 if rel else -1.0, accum_out=sums[:, t:t + 1]).then_inc(exp_done, 1)

            def evacuate(u, par, t):
                if window and t % 2 == 0:
                    return
                c, g = divmod(t, G)
                act.wait_ge(turned, TURNS * (TILES * u + t + 1))
                if g == (1 if window else 0) or (rotary and g == 1):
                    pts_free(act, u, par, t)
                k0 = 0 if window else BANK
                nc.scalar.copy(PTS[:, pts_slot(par, t), k0:k0 + BANK], PT[:, 1, :]).then_inc(evac_act, 1)

            def outputs(u, half):
                act.wait_ge(pv_done, CHUNKS * u + 4 * half + 4)
                nc.scalar.copy(OSB[:], O[:]).then_inc(o_out, 1)

            def prologue():
                for j in range(NJ):
                    prep(0, 0, j)

            def body(u, par, first, last):
                exponential(u, 0)
                for t in range(TILES):
                    if t + 1 < TILES:
                        exponential(u, t + 1)
                    if t == 2 and not first:
                        outputs(u - 1, 1)
                    if t - 1 in TAIL_AFTER and not first:
                        tail(u - 1, *TAIL_AFTER[t - 1])
                    if t - 1 in job_at and not last:
                        prep(u + 1, 1 - par, job_at[t - 1])
                    if t - 1 in TAIL_AT:
                        tail(u, *TAIL_AT[t - 1])
                    if t == (20 if rotary else 18):
                        outputs(u, 0)
                    evacuate(u, par, t)

            def epilogue():
                n = UNITS - 1
                outputs(n, 1)
                tail(n, 1, 1)
                tail(n, 1, 2)

            pairs(act, prologue, body, epilogue)


def program(nc, a, out):
    def scratch(n):
        return nc.dram_tensor(n, (IMAGES, HALF, 2, TOKENS), F32).ap()

    xn = scratch("xn_scratch")
    streams = [scratch(f"stream{i}") for i in range(3)] + [out]
    x = a["x"]
    sems = ExitStack()
    for i, kind in enumerate(("rel", "window", "rel", "rotary")):
        pre = f"L{i}_"
        w = {n[3:]: ap for n, ap in a.items() if n.startswith(pre)}
        lepe = {"wv": w["wv_all"], "bv": w["bv_all"], "lw": w["lw"], "lb": w["lb"], "wo": w["wo_all"]} if i == 3 else None
        normalise_block(nc, sems, f"n{i}", x, xn, streams[i], w["bo"], a["gavg"], lepe)
        attend_block(nc, sems, f"a{i}", kind, xn, streams[i], w, a["ident"])
        x = streams[i]
    sems.close()


def _halves(w):
    return w.reshape(2, HALF, -1).transpose(1, 0, 2)


def _by_group(w):
    return _halves(w).reshape(HALF, 2, GROUPS, G * DIM).transpose(2, 0, 1, 3)


def _spread_heads(w):
    z = np.zeros(w.shape[:-1] + (G, Q), w.dtype)
    z[..., 0:DIM] = w.reshape(w.shape[:-1] + (G, DIM))
    return z.reshape(w.shape[:-1] + (P,))


def _turn_pairs(w):
    return w.reshape(w.shape[:-1] + (-1, 2))[..., ::-1].reshape(w.shape)


def _layouts(inp):
    f = np.float32
    a = {}
    a["x"] = inp["x"].reshape(IMAGES, TOKENS, 2, HALF).transpose(0, 3, 2, 1)
    a["ident"] = np.eye(P, dtype=f)
    group = np.arange(HALF) // 6
    a["gavg"] = ((group[:, None] == group[None, :]) / 6.0).astype(f)

    qkv = {0: inp["L0_conv_w_qkv"], 1: inp["L1_conv_qkv_w"].T, 2: inp["L2_conv_qkv_w"].T,
           3: [inp[f"L3_conv_w{n}"].T for n in "qkv"]}
    bias = {0: inp["L0_conv_b_qkv"], 1: inp["L1_conv_qkv_b"], 2: inp["L2_conv_qkv_b"],
            3: [inp[f"L3_conv_b{n}"] for n in "qkv"]}
    wo = {0: inp["L0_conv_w_proj"], 1: inp["L1_conv_out_w"].T, 2: inp["L2_conv_proj_w"].T, 3: inp["L3_conv_wo"].T}
    bo = {0: inp["L0_conv_b_proj"], 1: inp["L1_conv_out_b"], 2: inp["L2_conv_proj_b"], 3: inp["L3_conv_bo"]}
    for i in range(4):
        if i == 3:
            (wq, wk, wv), (bq, bk, bv) = qkv[3], bias[3]
        else:
            wq, wk, wv = (qkv[i][:, n * CHANNELS:(n + 1) * CHANNELS] for n in range(3))
            bq, bk, bv = (bias[i][n * CHANNELS:(n + 1) * CHANNELS] for n in range(3))
        def by(b):
            return b.reshape(GROUPS, G * DIM)
        p = f"L{i}_"
        a[p + "wv"], a[p + "bv"] = _by_group(wv), by(bv)[:, :, None]
        a[p + "wo"] = _spread_heads(wo[i].T.reshape(CHANNELS, GROUPS, G * DIM).transpose(1, 0, 2)).transpose(0, 2, 1)
        a[p + "bo"] = bo[i].reshape(2, HALF).T
        if i in (0, 2):
            a[p + "wqk"] = np.concatenate([_by_group(wq), _by_group(wk)], axis=-1)
            a[p + "bqk"] = np.concatenate([by(bq), by(bk)], axis=-1)[:, :, None]
            rh = inp[f"L{i}_conv_rel_pos_h"][::-1].T
            rw = inp[f"L{i}_conv_rel_pos_w"][::-1].T
            a[p + "tab_h"], a[p + "tab_w"] = rh, rw
            key, line = np.arange(TOKENS)[None, :], np.arange(Q)[:, None]
            by_row, by_col = (key // SIDE == line).astype(f), (key % SIDE == line).astype(f)
            a[p + "ones"] = np.concatenate([np.zeros((96, TOKENS), f),
                                            (key // SIDE % DIM == line % DIM).astype(f)])
            a[p + "ones_rel"] = np.concatenate([by_col, by_col, by_col, by_row])
        else:
            for n, turned in (("qk", lambda t: t), ("qkr", _turn_pairs)):
                if n == "qk" or i == 3:
                    a[p + "w" + n] = np.concatenate([_by_group(turned(wq)), _by_group(turned(wk))], axis=-1)
                    a[p + "b" + n] = np.concatenate([by(turned(bq)), by(turned(bk))], axis=-1)[:, :, None]
        if i == 1:
            regs = np.zeros((CHANNELS, P), f)
            regs[:, 0:REGS] = inp["L1_conv_registers"].T
            a[p + "regs"] = _halves(regs)
            mask = np.full((P, 3, KEYS_W), -1e30, f)
            for n, c, k0 in ((0, 0, 0), (1, 1, 0), (2, CHUNKS - 1, CHUNKS - 3)):
                q, k = P * c + np.arange(P), P * k0 + np.arange(3 * P)
                ok = np.ones((P, 3 * P), bool)
                for qi, ki in ((q // SIDE, k // SIDE), (q % SIDE, k % SIDE)):
                    start = np.clip(qi - WINDOW // 2, 0, SIDE - WINDOW)[:, None]
                    ok &= (ki[None, :] >= start) & (ki[None, :] < start + WINDOW)
                mask[:, n, 0:3 * P][ok] = 0
                mask[:, n, 3 * P:3 * P + REGS] = 0
            a[p + "mask"] = mask
        if i == 3:
            a[p + "wv_all"], a[p + "bv_all"] = _halves(wv), bv.reshape(2, HALF).T
            a[p + "wo_all"] = _halves(wo[3])
            a[p + "lw"] = inp["L3_conv_lepe_w"].reshape(TAPS * TAPS, 2, HALF).transpose(2, 1, 0)
            a[p + "lb"] = inp["L3_conv_lepe_b"].reshape(2, HALF).T
            for n in ("sin", "cos"):
                a[p + n] = np.tile(inp[f"L3_conv_{n}"].reshape(TOKENS, DIM).T, (P // DIM, 1))
            a[p + "sign"] = np.where(np.arange(P) % 2, 1.0, -1.0).astype(f)[:, None]
            a[p + "mask"] = inp["L3_conv_mask"].reshape(GROUPS, G, CHUNKS, P, TOKENS).transpose(0, 2, 3, 1, 4)
    return {n: np.ascontiguousarray(v) for n, v in a.items()}


def kernel(**inputs):
    import concourse.bacc as _bacc
    from concourse.bass_utils import run_bass_kernel_spmd as _run

    arrays = _layouts({n: np.asarray(v) for n, v in inputs.items()})
    nc = _bacc.Bacc("TRN2", target_bir_lowering=False, num_devices=1)
    aps = {n: nc.dram_tensor(n, v.shape, mybir.dt.from_np(v.dtype), kind="ExternalInput").ap() for n, v in arrays.items()}
    out = nc.dram_tensor("out", (IMAGES, HALF, 2, TOKENS), F32, kind="ExternalOutput").ap()
    program(nc, aps, out)
    r = _run(nc, [arrays], core_ids=[0])
    y = r.results[0]["out"]
    return y.transpose(0, 3, 2, 1).reshape(IMAGES, SIDE, SIDE, CHANNELS)
```
